# Optimizing a Trainium2 kernel written in Bass

```python
import numpy as np
import jax
import jax.numpy as jnp

def _softmax(x, axis=-1):
    return jax.nn.softmax(x, axis=axis)

def _gelu(x):
    return jax.nn.gelu(x, approximate=True)

def _silu(x):
    return jax.nn.silu(x)

def _sigmoid(x):
    return jax.nn.sigmoid(x)

def _layernorm(x, axis=-1, eps=1e-05):
    m = jnp.mean(x, axis=axis, keepdims=True)
    v = jnp.var(x, axis=axis, keepdims=True)
    return (x - m) / jnp.sqrt(v + eps)

def _scatter_add(tgt, idx, src, axis=0):
    return tgt.at[idx].add(src)

def _segment_sum(src, seg, n):
    return jax.ops.segment_sum(src, seg, n)
kernel_name = 'mk_decoder_preln_d2_seqx_r8_d50dd4'

def setup_inputs(seed: int=0):
    np.random.seed(seed)
    _w = jnp.asarray

    def _rec_inputs():
        import jax
        import jax.numpy as jnp
        _rk = jax.random.key(seed)
        x = -0.000125 + 0.9999 * jax.random.normal(jax.random.fold_in(_rk, 1), (1, 1024, 128), jnp.float32)
        _lenS = 1024 - jax.random.randint(jax.random.fold_in(_rk, 7), (1,), 0, max(1, 1024 // 4) + 1, jnp.int32)
        _lenS2 = 6404 - jax.random.randint(jax.random.fold_in(_rk, 8), (1,), 0, max(1, 6404 // 4) + 1, jnp.int32)
        _ctx_768P = jax.random.normal(jax.random.fold_in(_rk, 11), (1, 16, 96), jnp.float32)
        _ctx_768c = jax.random.dirichlet(jax.random.fold_in(_rk, 511), 0.3 * jnp.ones((16,), jnp.float32), (1, 6404))
        _ctx_768t = jnp.einsum('bsk,bkd->bsd', _ctx_768c, _ctx_768P)
        _ctx_768t = _ctx_768t * jax.lax.rsqrt(jnp.mean(jnp.square(_ctx_768t)) + 1e-12) * 0.953939
        ctx_768 = 0.00272024 + 0.999456 * (_ctx_768t + 0.3 * jax.random.normal(jax.random.fold_in(_rk, 611), (1, 6404, 96), jnp.float32))
        return (x, ctx_768)
    x, ctx_768 = _rec_inputs()

    def _L0_attn_setup():
        import jax, jax.numpy as jnp
        import numpy as np
        HEAD_SIZE = 64
        key = jax.random.key(seed)
        ks = jax.random.split(key, 5)
        B, N, D, H, E, O = (2, 256, 128, 16, HEAD_SIZE, 128)
        return {'query': jax.random.normal(ks[0], (B, N, D), dtype=jnp.float32), 'Wq': jax.random.normal(ks[1], (H, D, E), dtype=jnp.float32) / np.sqrt(D), 'Wk': jax.random.normal(ks[2], (H, D, E), dtype=jnp.float32) / np.sqrt(D), 'Wv': jax.random.normal(ks[3], (H, D, E), dtype=jnp.float32) / np.sqrt(D), 'Wp': jax.random.normal(ks[4], (H * E, O), dtype=jnp.float32) / np.sqrt(H * E), 'bp': jnp.zeros((O,), dtype=jnp.float32)}
    _L0_attn_all = _L0_attn_setup()
    _L0_attn_in = {k: v for k, v in _L0_attn_all.items() if k in ('Wq', 'Wk', 'Wv', 'Wp', 'bp')}
    del _L0_attn_all

    def _L0_xattn_setup():
        import jax, jax.numpy as jnp
        import numpy as np
        HEADS = 16
        DIM_HEAD = 64
        SCALE = DIM_HEAD ** (-0.5)
        QUERY_DIM = 128
        CONTEXT_DIM = 96
        INNER_DIM = HEADS * DIM_HEAD
        key = jax.random.key(seed)
        ks = jax.random.split(key, 7)
        B, Nq, Nk = (8, 512, 77)
        x = jax.random.normal(ks[0], (B, Nq, QUERY_DIM), dtype=jnp.float32)
        context = jax.random.normal(ks[1], (B, Nk, CONTEXT_DIM), dtype=jnp.float32)
        Wq = jax.random.normal(ks[2], (QUERY_DIM, INNER_DIM), dtype=jnp.float32) * QUERY_DIM ** (-0.5)
        Wk = jax.random.normal(ks[3], (CONTEXT_DIM, INNER_DIM), dtype=jnp.float32) * CONTEXT_DIM ** (-0.5)
        Wv = jax.random.normal(ks[4], (CONTEXT_DIM, INNER_DIM), dtype=jnp.float32) * CONTEXT_DIM ** (-0.5)
        Wo = jax.random.normal(ks[5], (INNER_DIM, QUERY_DIM), dtype=jnp.float32) * INNER_DIM ** (-0.5)
        bo = jnp.zeros((QUERY_DIM,), dtype=jnp.float32)
        return {'x': x, 'context': context, 'Wq': Wq, 'Wk': Wk, 'Wv': Wv, 'Wo': Wo, 'bo': bo}
    _L0_xattn_all = _L0_xattn_setup()
    _L0_xattn_in = {k: v for k, v in _L0_xattn_all.items() if k in ('Wq', 'Wk', 'Wv', 'Wo', 'bo')}
    del _L0_xattn_all

    def _L0_ffn_setup():
        import jax, jax.numpy as jnp
        import numpy as np
        TOP_K = 2

        def _mlp(x, w1, b1, w2, b2):
            h = jax.nn.gelu(jnp.einsum('bsd,di->bsi', x, w1) + b1)
            return jnp.einsum('bsi,id->bsd', h, w2) + b2
        key = jax.random.key(seed)
        ks = jax.random.split(key, 8)
        B, S, D, I, E = (2, 256, 128, 512, 8)
        s_in = 1.0 / np.sqrt(D)
        s_mid = 1.0 / np.sqrt(I)
        return {'x': jax.random.normal(ks[0], (B, S, D), jnp.float32), 'gate_w': jax.random.normal(ks[1], (D, E), jnp.float32) * s_in, 'gate_b': jnp.zeros((E,), jnp.float32), 'sh_w1': jax.random.normal(ks[2], (D, I), jnp.float32) * s_in, 'sh_b1': jnp.zeros((I,), jnp.float32), 'sh_w2': jax.random.normal(ks[3], (I, D), jnp.float32) * s_mid, 'sh_b2': jnp.zeros((D,), jnp.float32), 'ew1': jax.random.normal(ks[4], (E, D, I), jnp.float32) * s_in, 'eb1': jnp.zeros((E, I), jnp.float32), 'ew2': jax.random.normal(ks[5], (E, I, D), jnp.float32) * s_mid, 'eb2': jnp.zeros((E, D), jnp.float32)}
    _L0_ffn_all = _L0_ffn_setup()
    _L0_ffn_in = {k: v for k, v in _L0_ffn_all.items() if k in ('gate_w', 'gate_b', 'sh_w1', 'sh_b1', 'sh_w2', 'sh_b2', 'ew1', 'eb1', 'ew2', 'eb2')}
    del _L0_ffn_all

    def _L1_attn_setup():
        import jax, jax.numpy as jnp
        import numpy as np
        B, N, DIM, H = (2, 256, 128, 16)
        DH = DIM // H
        SCALE = DH ** (-0.5)

        def _rotary_emb(n, d, dtype):
            inv_freq = 1.0 / 10000.0 ** (jnp.arange(0, d, 2, dtype=jnp.float32) / d)
            freqs = jnp.outer(jnp.arange(n, dtype=jnp.float32), inv_freq)
            return jnp.concatenate([freqs, freqs], axis=-1).astype(dtype)

        def _rotate_half(x):
            x1, x2 = jnp.split(x, 2, axis=-1)
            return jnp.concatenate([-x2, x1], axis=-1)

        def _apply_rotary(freqs, t):
            return t * jnp.cos(freqs) + _rotate_half(t) * jnp.sin(freqs)
        key = jax.random.key(seed)
        ks = jax.random.split(key, 4)
        x = jax.random.normal(ks[0], (B, N, DIM), dtype=jnp.float32)
        Wq = jax.random.normal(ks[1], (DIM, DIM), dtype=jnp.float32) * DIM ** (-0.5)
        Wkv = jax.random.normal(ks[2], (DIM, DIM), dtype=jnp.float32) * DIM ** (-0.5)
        Wout = jax.random.normal(ks[3], (DIM, DIM), dtype=jnp.float32) * DIM ** (-0.5)
        bout = jnp.zeros((DIM,), dtype=jnp.float32)
        return {'x': x, 'Wq': Wq, 'Wkv': Wkv, 'Wout': Wout, 'bout': bout}
    _L1_attn_all = _L1_attn_setup()
    _L1_attn_in = {k: v for k, v in _L1_attn_all.items() if k in ('Wq', 'Wkv', 'Wout', 'bout')}
    del _L1_attn_all

    def _L1_xattn_setup():
        import jax, jax.numpy as jnp
        import numpy as np
        QUERY_DIM = 128
        CONTEXT_DIM = 96
        HEADS = 8
        DIM_HEAD = 64
        INNER = HEADS * DIM_HEAD
        key = jax.random.key(seed)
        ks = jax.random.split(key, 7)
        B, S, L = (8, 512, 77)
        x = jax.random.normal(ks[0], (B, S, QUERY_DIM), dtype=jnp.float32)
        context = jax.random.normal(ks[1], (B, L, CONTEXT_DIM), dtype=jnp.float32)
        Wq = jax.random.normal(ks[2], (QUERY_DIM, INNER), dtype=jnp.float32) * QUERY_DIM ** (-0.5)
        Wk = jax.random.normal(ks[3], (CONTEXT_DIM, INNER), dtype=jnp.float32) * CONTEXT_DIM ** (-0.5)
        Wv = jax.random.normal(ks[4], (CONTEXT_DIM, INNER), dtype=jnp.float32) * CONTEXT_DIM ** (-0.5)
        Wo = jax.random.normal(ks[5], (INNER, QUERY_DIM), dtype=jnp.float32) * INNER ** (-0.5)
        bo = jax.random.normal(ks[6], (QUERY_DIM,), dtype=jnp.float32) * 0.01
        return {'x': x, 'context': context, 'Wq': Wq, 'Wk': Wk, 'Wv': Wv, 'Wo': Wo, 'bo': bo}
    _L1_xattn_all = _L1_xattn_setup()
    _L1_xattn_in = {k: v for k, v in _L1_xattn_all.items() if k in ('Wq', 'Wk', 'Wv', 'Wo', 'bo')}
    del _L1_xattn_all

    def _L1_ffn_setup():
        import jax, jax.numpy as jnp
        import numpy as np
        E, K, D, F = (8, 2, 128, 512)
        EPS = 1e-06
        B, S = (2, 128)
        key = jax.random.key(seed)
        ks = jax.random.split(key, 6)
        s_in = 1.0 / np.sqrt(D)
        s_mid = 1.0 / np.sqrt(F)
        return {'x': jax.random.normal(ks[0], (B, S, D), dtype=jnp.float32), 'Wg': jax.random.normal(ks[1], (D, E), dtype=jnp.float32) * s_in, 'gamma': jnp.ones((E, D), dtype=jnp.float32), 'beta': jnp.zeros((E, D), dtype=jnp.float32), 'W1': jax.random.normal(ks[2], (E, D, F), dtype=jnp.float32) * s_in, 'b1': jnp.zeros((E, F), dtype=jnp.float32), 'W2': jax.random.normal(ks[3], (E, F, D), dtype=jnp.float32) * s_mid, 'b2': jnp.zeros((E, D), dtype=jnp.float32)}
    _L1_ffn_all = _L1_ffn_setup()
    _L1_ffn_in = {k: v for k, v in _L1_ffn_all.items() if k in ('Wg', 'gamma', 'beta', 'W1', 'b1', 'W2', 'b2')}
    del _L1_ffn_all
    return {'x': x, 'ctx_768': ctx_768, 'L0_attn_Wq': _L0_attn_in['Wq'], 'L0_attn_Wk': _L0_attn_in['Wk'], 'L0_attn_Wv': _L0_attn_in['Wv'], 'L0_attn_Wp': _L0_attn_in['Wp'], 'L0_attn_bp': _L0_attn_in['bp'], 'L0_xattn_Wq': _L0_xattn_in['Wq'], 'L0_xattn_Wk': _L0_xattn_in['Wk'], 'L0_xattn_Wv': _L0_xattn_in['Wv'], 'L0_xattn_Wo': _L0_xattn_in['Wo'], 'L0_xattn_bo': _L0_xattn_in['bo'], 'L0_ffn_gate_w': _L0_ffn_in['gate_w'], 'L0_ffn_gate_b': _L0_ffn_in['gate_b'], 'L0_ffn_sh_w1': _L0_ffn_in['sh_w1'], 'L0_ffn_sh_b1': _L0_ffn_in['sh_b1'], 'L0_ffn_sh_w2': _L0_ffn_in['sh_w2'], 'L0_ffn_sh_b2': _L0_ffn_in['sh_b2'], 'L0_ffn_ew1': _L0_ffn_in['ew1'], 'L0_ffn_eb1': _L0_ffn_in['eb1'], 'L0_ffn_ew2': _L0_ffn_in['ew2'], 'L0_ffn_eb2': _L0_ffn_in['eb2'], 'L1_attn_Wq': _L1_attn_in['Wq'], 'L1_attn_Wkv': _L1_attn_in['Wkv'], 'L1_attn_Wout': _L1_attn_in['Wout'], 'L1_attn_bout': _L1_attn_in['bout'], 'L1_xattn_Wq': _L1_xattn_in['Wq'], 'L1_xattn_Wk': _L1_xattn_in['Wk'], 'L1_xattn_Wv': _L1_xattn_in['Wv'], 'L1_xattn_Wo': _L1_xattn_in['Wo'], 'L1_xattn_bo': _L1_xattn_in['bo'], 'L1_ffn_Wg': _L1_ffn_in['Wg'], 'L1_ffn_gamma': _L1_ffn_in['gamma'], 'L1_ffn_beta': _L1_ffn_in['beta'], 'L1_ffn_W1': _L1_ffn_in['W1'], 'L1_ffn_b1': _L1_ffn_in['b1'], 'L1_ffn_W2': _L1_ffn_in['W2'], 'L1_ffn_b2': _L1_ffn_in['b2']}

def reference(x, ctx_768, L0_attn_Wq, L0_attn_Wk, L0_attn_Wv, L0_attn_Wp, L0_attn_bp, L0_xattn_Wq, L0_xattn_Wk, L0_xattn_Wv, L0_xattn_Wo, L0_xattn_bo, L0_ffn_gate_w, L0_ffn_gate_b, L0_ffn_sh_w1, L0_ffn_sh_b1, L0_ffn_sh_w2, L0_ffn_sh_b2, L0_ffn_ew1, L0_ffn_eb1, L0_ffn_ew2, L0_ffn_eb2, L1_attn_Wq, L1_attn_Wkv, L1_attn_Wout, L1_attn_bout, L1_xattn_Wq, L1_xattn_Wk, L1_xattn_Wv, L1_xattn_Wo, L1_xattn_bo, L1_ffn_Wg, L1_ffn_gamma, L1_ffn_beta, L1_ffn_W1, L1_ffn_b1, L1_ffn_W2, L1_ffn_b2):
    import jax
    import jax.numpy as jnp

    def _L0_attn_ref(query, Wq, Wk, Wv, Wp, bp):
        import jax, jax.numpy as jnp
        import numpy as np
        HEAD_SIZE = 64
        B, N, D = query.shape
        H, _, E = Wq.shape
        scale = 1.0 / jnp.sqrt(jnp.asarray(E, query.dtype))
        q = jnp.einsum('bnd,hde->bhne', query, Wq) * scale
        k = jnp.einsum('bmd,hde->bhme', query, Wk)
        v = jnp.einsum('bmd,hde->bhme', query, Wv)
        logits = jnp.einsum('bhne,bhme->bhnm', q, k)
        attn = jax.nn.softmax(logits, axis=-1)
        out = jnp.einsum('bhnm,bhme->bnhe', attn, v)
        out = jnp.swapaxes(out, -1, -2).reshape(B, N, E * H)
        return jnp.dot(out, Wp) + bp

    def _L0_xattn_ref(x, context, Wq, Wk, Wv, Wo, bo):
        import jax, jax.numpy as jnp
        import numpy as np
        HEADS = 16
        DIM_HEAD = 64
        SCALE = DIM_HEAD ** (-0.5)
        QUERY_DIM = 128
        CONTEXT_DIM = 96
        INNER_DIM = HEADS * DIM_HEAD
        B, Nq, _ = x.shape
        Nk = context.shape[1]
        q = x @ Wq
        k = context @ Wk
        v = context @ Wv
        q = q.reshape(B, Nq, HEADS, DIM_HEAD).transpose(0, 2, 1, 3)
        k = k.reshape(B, Nk, HEADS, DIM_HEAD).transpose(0, 2, 1, 3)
        v = v.reshape(B, Nk, HEADS, DIM_HEAD).transpose(0, 2, 1, 3)
        sim = jnp.einsum('bhid,bhjd->bhij', q, k) * SCALE
        attn = jax.nn.softmax(sim, axis=-1)
        out = jnp.einsum('bhij,bhjd->bhid', attn, v)
        out = out.transpose(0, 2, 1, 3).reshape(B, Nq, INNER_DIM)
        return out @ Wo + bo

    def _L0_ffn_ref(x, gate_w, gate_b, sh_w1, sh_b1, sh_w2, sh_b2, ew1, eb1, ew2, eb2):
        import jax, jax.numpy as jnp
        import numpy as np
        TOP_K = 2

        def _mlp(x, w1, b1, w2, b2):
            h = jax.nn.gelu(jnp.einsum('bsd,di->bsi', x, w1) + b1)
            return jnp.einsum('bsi,id->bsd', h, w2) + b2
        E = ew1.shape[0]
        router_probs = jax.nn.softmax(jnp.einsum('bsd,de->bse', x, gate_w) + gate_b, axis=-1)
        expert_values, expert_indices = jax.lax.top_k(router_probs, k=TOP_K)
        expert_values = expert_values / (jnp.sum(expert_values, axis=-1, keepdims=True) + 1e-09)
        h = jax.nn.gelu(jnp.einsum('bsd,edi->bsei', x, ew1) + eb1)
        all_outputs = jnp.einsum('bsei,eid->bsed', h, ew2) + eb2
        one_hot = jax.nn.one_hot(expert_indices, E, dtype=x.dtype)
        weights_E = (one_hot * expert_values[..., None]).sum(axis=2)
        moe_out = jnp.einsum('bse,bsed->bsd', weights_E, all_outputs)
        return x + _mlp(x, sh_w1, sh_b1, sh_w2, sh_b2) + moe_out

    def _L1_attn_ref(x, Wq, Wkv, Wout, bout):
        import jax, jax.numpy as jnp
        import numpy as np
        B, N, DIM, H = (2, 256, 128, 16)
        DH = DIM // H
        SCALE = DH ** (-0.5)

        def _rotary_emb(n, d, dtype):
            inv_freq = 1.0 / 10000.0 ** (jnp.arange(0, d, 2, dtype=jnp.float32) / d)
            freqs = jnp.outer(jnp.arange(n, dtype=jnp.float32), inv_freq)
            return jnp.concatenate([freqs, freqs], axis=-1).astype(dtype)

        def _rotate_half(x):
            x1, x2 = jnp.split(x, 2, axis=-1)
            return jnp.concatenate([-x2, x1], axis=-1)

        def _apply_rotary(freqs, t):
            return t * jnp.cos(freqs) + _rotate_half(t) * jnp.sin(freqs)
        b, n, dim = x.shape
        q = x @ Wq
        kv = x @ Wkv
        split = lambda t: t.reshape(b, n, H, DH).transpose(0, 2, 1, 3).reshape(b * H, n, DH)
        q, kv = (split(q), split(kv))
        freqs = _rotary_emb(n, DH, x.dtype)[None]
        q = _apply_rotary(freqs, q)
        kv = _apply_rotary(freqs, kv)
        q = q * SCALE
        att = jnp.einsum('bmd,bnd->bmn', q, kv)
        attn = jax.nn.softmax(att, axis=-1)
        out = jnp.einsum('bij,bjd->bid', attn, kv)
        out = out.reshape(b, H, n, DH).transpose(0, 2, 1, 3).reshape(b, n, dim)
        return out @ Wout + bout

    def _L1_xattn_ref(x, context, Wq, Wk, Wv, Wo, bo):
        import jax, jax.numpy as jnp
        import numpy as np
        QUERY_DIM = 128
        CONTEXT_DIM = 96
        HEADS = 8
        DIM_HEAD = 64
        INNER = HEADS * DIM_HEAD
        B, S, _ = x.shape
        L = context.shape[1]
        scale = DIM_HEAD ** (-0.5)
        q = (x @ Wq).reshape(B, S, HEADS, DIM_HEAD).transpose(0, 2, 1, 3)
        k = (context @ Wk).reshape(B, L, HEADS, DIM_HEAD).transpose(0, 2, 1, 3)
        v = (context @ Wv).reshape(B, L, HEADS, DIM_HEAD).transpose(0, 2, 1, 3)
        attn = jnp.einsum('bhsd,bhld->bhsl', q, k) * scale
        attn = jax.nn.softmax(attn, axis=-1)
        out = jnp.einsum('bhsl,bhld->bhsd', attn, v)
        out = out.transpose(0, 2, 1, 3).reshape(B, S, INNER)
        return out @ Wo + bo

    def _L1_ffn_ref(x, Wg, gamma, beta, W1, b1, W2, b2):
        import jax, jax.numpy as jnp
        import numpy as np
        E, K, D, F = (8, 2, 128, 512)
        EPS = 1e-06
        B, S = (2, 128)
        orig_shape = x.shape
        xf = x.reshape(-1, orig_shape[-1])
        scores = xf @ Wg
        w, idx = jax.lax.top_k(scores, K)
        w = jax.nn.softmax(w, axis=-1)
        mu = jnp.mean(xf, axis=-1, keepdims=True)
        var = jnp.var(xf, axis=-1, keepdims=True)
        xhat = (xf - mu) * jax.lax.rsqrt(var + EPS)
        normed = xhat[None, :, :] * gamma[:, None, :] + beta[:, None, :]
        h = jax.nn.relu(jnp.einsum('end,edf->enf', normed, W1) + b1[:, None, :])
        out = jnp.einsum('enf,efd->end', h, W2) + b2[:, None, :] + xf[None, :, :]
        cw = jnp.sum(w[..., None] * jax.nn.one_hot(idx, E, dtype=w.dtype), axis=1)
        y = jnp.einsum('ne,end->nd', cw, out)
        return y.reshape(orig_shape)
    x = x + _L0_attn_ref(_layernorm(x, axis=-1), L0_attn_Wq, L0_attn_Wk, L0_attn_Wv, L0_attn_Wp, L0_attn_bp)
    x = x + _L0_xattn_ref(_layernorm(x, axis=-1), ctx_768, L0_xattn_Wq, L0_xattn_Wk, L0_xattn_Wv, L0_xattn_Wo, L0_xattn_bo)
    x = x + _L0_ffn_ref(_layernorm(x, axis=-1), L0_ffn_gate_w, L0_ffn_gate_b, L0_ffn_sh_w1, L0_ffn_sh_b1, L0_ffn_sh_w2, L0_ffn_sh_b2, L0_ffn_ew1, L0_ffn_eb1, L0_ffn_ew2, L0_ffn_eb2)
    x = x + _L1_attn_ref(_layernorm(x, axis=-1), L1_attn_Wq, L1_attn_Wkv, L1_attn_Wout, L1_attn_bout)
    x = x + _L1_xattn_ref(_layernorm(x, axis=-1), ctx_768, L1_xattn_Wq, L1_xattn_Wk, L1_xattn_Wv, L1_xattn_Wo, L1_xattn_bo)
    x = x + _L1_ffn_ref(_layernorm(x, axis=-1), L1_ffn_Wg, L1_ffn_gamma, L1_ffn_beta, L1_ffn_W1, L1_ffn_b1, L1_ffn_W2, L1_ffn_b2)
    return x

_drawn_inputs = setup_inputs


def setup_inputs(seed=0):
    import zlib

    import numpy as np

    out = dict(_drawn_inputs(seed))
    spreads = {'L0_attn_bp': (0.0, 0.1),
     'L0_xattn_bo': (0.0, 0.1),
     'L0_ffn_gate_b': (0.0, 0.1),
     'L0_ffn_sh_b1': (0.0, 0.1),
     'L0_ffn_sh_b2': (0.0, 0.1),
     'L0_ffn_eb1': (0.0, 0.29),
     'L0_ffn_eb2': (0.0, 0.1),
     'L1_attn_bout': (0.0, 0.1),
     'L1_ffn_gamma': (1.0, 0.548),
     'L1_ffn_beta': (0.0, 0.538),
     'L1_ffn_b1': (0.0, 0.54),
     'L1_ffn_b2': (0.0, 0.367)}
    factors = {'L1_xattn_bo': 5.615}
    for name, (base, spread) in spreads.items():
        noise = np.random.default_rng([zlib.crc32(name.encode()), seed]).standard_normal(out[name].shape)
        drawn = base * np.exp(spread * noise) if base else spread * noise
        out[name] = jnp.asarray(drawn.astype(out[name].dtype))
    for name, factor in factors.items():
        out[name] = (out[name] * factor).astype(out[name].dtype)
    return out
```

```python
from contextlib import ExitStack

import numpy as np

import concourse.bass as bass
from concourse import mybir

F32 = mybir.dt.float32
F32R = mybir.dt.float32r
ALU = mybir.AluOpType
ACT = mybir.ActivationFunctionType
AX = mybir.AxisListType

P = 128
N = 1024
D = 128
NT = N // P
HALF = 512
CHUNK = 512
E = 64
LO0 = 64
VW = 2 * E + 1
SLOTS = 4
LAG = 3
EVAC_STEP = LAG
POST_STEP = LAG + 2


class Head:

    def __init__(self, h, par, hp):
        self.h, self.par, self.hp = h, par, hp
        self.first = isinstance(h, int) and h == 0
        self.early = isinstance(h, int) and h < 2

    def back(self, n):
        if n == 2:
            return Head(self.h - 2, self.par, self.hp - 1)
        return Head(self.h - 1, 1 - self.par, self.hp - (1 - self.par))


def static_head(h):
    return Head(h, h % 2, h // 2)


def over_heads(eng, heads, period):
    period(static_head(0), static_head(1), False)
    with eng.Fori(0, (heads - 2) // 2) as it:
        odd, even, odd2 = Head(1 + 2 * it, 1, it), Head(2 + 2 * it, 0, it + 1), Head(3 + 2 * it, 1, it + 1)
        period(odd, even, False)
        period(even, odd2, False)
    period(static_head(heads - 1), None, True)


class Plan:

    def __init__(self, keys, packed):
        self.keys = keys
        self.tiles = -(-keys // P)
        self.chunks = -(-keys // CHUNK)
        self.units = 2 * self.tiles
        max_jobs = [[("X", t, c) for t in range(NT)] for c in range(self.chunks)]
        if packed:
            seq = [j for c in max_jobs for j in c]
        else:
            seq = [("Q", 0), ("Q", 1)]
            for c in range(self.chunks):
                seq += [("K", c), ("V", c)] + (max_jobs[c - 1] if c else [])
            seq += max_jobs[-1]
        self.prep = seq + [("M", 0), ("M", 1)]
        steps = [[] for _ in range(self.units)]
        first, last = POST_STEP, self.units - 4
        for k, job in enumerate(seq):
            steps[first + k * (last - first + 1) // len(seq)].append(job)
        steps[self.units - 2] += [("M", 0), ("M", 1)]
        steps[POST_STEP] = [("D", 1), ("Y", 1)] + steps[POST_STEP]
        steps[self.tiles + POST_STEP] = [("D", 0), ("Y", 0)] + steps[self.tiles + POST_STEP]
        self.steps = steps
        order = [j for s in steps for j in s]
        self.local = {j: n for n, j in enumerate(order)}
        self.per_head = len(order)
        self.lead = len(self.prep) - 2

    def job(self, head, job):
        return self.lead + head.h * self.per_head + self.local[job]

    def prep_job(self, head, job):
        if head.first:
            return self.prep.index(job)
        return self.job(head.back(1), job)

    def post_job(self, head, half, kind, heads):
        if half == 0:
            if isinstance(head.h, int) and head.h == heads - 1:
                return self.lead + head.h * self.per_head + 2 + (kind == "Y")
            return self.job(head, (kind, 0))
        if isinstance(head.h, int) and head.h == heads - 1:
            return self.lead + head.h * self.per_head + 4 + (kind == "Y")
        return self.job(Head(head.h + 1, 1 - head.par, None), (kind, 1))

    def jobs_at(self, head, last, step):
        out = []
        for j in self.steps[step]:
            if j[0] in "DY":
                if j[1] == 1 and head.first:
                    continue
                if j[1] == 0 and last:
                    out.append((self.lead + head.h * self.per_head + 2 + (j[0] == "Y"), j))
                    continue
            elif last:
                continue
            out.append((self.job(head, j), j))
        return out

    def chunk_keys(self, c):
        return min(CHUNK, self.keys - c * CHUNK)

    def tile_keys(self, i):
        return min(P, self.keys - i * P)

    def unit(self, head, u):
        return head.h * self.units + u


def attention(nc, held, name, heads, keys, X, XT, ident, w, bias, ctx_dram=None, packed=None, scale=0.125):
    plan = Plan(keys, packed is not None)
    C = ctx_dram.shape[0] if ctx_dram is not None else P
    TILES, CHUNKS, UNITS = plan.tiles, plan.chunks, plan.units
    KW = TILES * P
    with ExitStack() as ctx:
        def sb(n, shape, dt=F32):
            return ctx.enter_context(nc.sbuf_tensor(f"{name}_{n}", shape, dt))

        def sem(n):
            return held.enter_context(nc.semaphore(f"{name}_{n}"))

        KA = [sb(f"KA{i}", [P, KW], F32R) for i in range(2)]
        KB = [sb(f"KB{i}", [P, KW], F32R) for i in range(2)]
        QA = [sb(f"QA{i}", [P, N], F32R) for i in range(2)]
        QB = [sb(f"QB{i}", [P, N], F32R) for i in range(2)]
        V = [sb(f"V{i}", [P, TILES, VW], F32R) for i in range(2)]
        HI = [sb(f"HI{i}", [P, HALF], F32R) for i in range(SLOTS)]
        LO = [sb(f"LO{i}", [P, HALF], F32R) for i in range(SLOTS)]
        SUM = [sb(f"SUM{i}", [P, HALF]) for i in range(2)]
        OT = sb("OT", [P, HALF])
        LOSUM = sb("LOSUM", [P, HALF])
        RDEN = sb("RDEN", [P, HALF // P])
        MX = sb("MX", [P, NT, CHUNKS])
        NEGMAX = sb("NEGMAX", [P, NT])
        SHIFT = sb("SHIFT", [P, NT], F32R)
        WO = [sb(f"WO{i}", [P, D]) for i in range(2)]
        ones = sb("ones", [P, 8])
        BIAS = sb("BIAS", [P, D])
        if packed is None:
            WQ = sb("WQ", [P, P])
            WK = sb("WK", [P, P])
            WV = sb("WV", [P, E])
        if ctx_dram is not None:
            CTX = [sb(f"CTX{i}", [P, CHUNK]) for i in range(2)]
        if packed is not None:
            VH, VL = packed["vh"], packed["vl"]

        def bank(n):
            return ctx.enter_context(nc.psum_tensor(f"{name}_{n}", [P, 512], F32))

        S = [bank(f"S{i}") for i in range(SLOTS)]
        OA, OB = bank("OA"), bank("OB")
        SIDE = [bank(f"SIDE{i}") for i in range(2)]

        filled = sem("filled")
        bias_in = sem("bias_in")
        bias_added = sem("bias_added")
        w_in = sem("w_in")
        wo_in = [sem(f"wo_in{i}") for i in range(2)]
        ctx_in = [sem(f"ctx_in{i}") for i in range(2)]
        kb_in = [sem(f"kb_in{i}") for i in range(2)]
        side_done = sem("side_done")
        side_act = sem("side_act")
        side_free = sem("side_free")
        s_done = sem("s_done")
        hi_done = sem("hi_done")
        p_done = sem("p_done")
        lo_done = sem("lo_done")
        pv_done = sem("pv_done")
        sum_done = sem("sum_done")
        evac = sem("evac")
        max_step = sem("max_step")

        ACT_PER_HEAD = 2 + 2 * CHUNKS
        act_order = [j for j in plan.prep if j[0] in "QKV"]

        def act_count(head, job):
            return head.h * ACT_PER_HEAD + act_order.index(job) + 1

        def sums_before(head, half, i):
            return (2 * head.h + half) * (TILES - 1) + max(i, 1)

        def ctx_slot(head, c):
            return (head.par * CHUNKS + c) % 2

        def ctx_count(head, c):
            return 16 * (CHUNKS * head.hp + (head.par * CHUNKS + c) // 2 + 1)

        KB_DMAS = CHUNKS if packed is None else 6

        def unit_slot(head, u):
            return (head.par * UNITS + u) % SLOTS

        assert 2 * UNITS % SLOTS == 0

        def v_parts(c):
            t0 = c * CHUNK // P
            t1 = min(t0 + CHUNK // P, TILES)
            full = keys // P
            out = [(P, t0, min(t1, full))] if min(t1, full) > t0 else []
            if t1 > full:
                out.append((keys - full * P, full, t1))
            return out

        def v_offset(c, t):
            return t - c * CHUNK // P

        def side_bank(head, n, job):
            if isinstance(n, int):
                return n % 2
            return bank_of[job]

        assert plan.per_head % 2 == 0
        bank_of = {j: (plan.lead + k) % 2 for j, k in plan.local.items()}

        with nc.Block() as block:

            @block.sync
            def _(sp):
                sp.dma_start(BIAS[:], bias.partition_broadcast(P)).then_inc(bias_in, 16)

                def load_wo(head, free):
                    if not head.early:
                        sp.wait_ge(side_done, free)
                    sp.dma_start(WO[head.par][:], w[3][head.h, :, :]).then_inc(wo_in[head.par], 16)

                def prepare(head):
                    par = head.par
                    if packed is None:
                        if not head.first:
                            sp.wait_ge(side_done, plan.prep_job(head.back(1), ("V", CHUNKS - 1)) + 1)
                        sp.dma_start(WQ[:], w[0][head.h, :, :]).then_inc(w_in, 16)
                        sp.dma_start(WK[0:C, :], w[1][head.h, :, :]).then_inc(w_in, 16)
                        sp.dma_start(WV[0:C, :], w[2][head.h, :, :]).then_inc(w_in, 16)

                        def load_ctx(c):
                            if c >= 2:
                                sp.wait_ge(side_done, plan.prep_job(head, ("V", c - 2)) + 1)
                            sp.dma_start(CTX[ctx_slot(head, c)][0:C, 0:plan.chunk_keys(c)],
                                         ctx_dram[:, c * CHUNK:c * CHUNK + plan.chunk_keys(c)])\
                              .then_inc(ctx_in[ctx_slot(head, c)], 16)

                        if ctx_dram is not None:
                            load_ctx(0)
                            load_ctx(1)
                        for c in range(CHUNKS):
                            sp.wait_ge(side_act, act_count(head, ("K", c)))
                            k = slice(c * CHUNK, c * CHUNK + plan.chunk_keys(c))
                            sp.dma_start(KB[par][0:E, k].bitcast(F32), KA[par][0:E, k].bitcast(F32)).then_inc(kb_in[par], 16)
                            if ctx_dram is not None and c + 2 < CHUNKS:
                                load_ctx(c + 2)
                    else:
                        if head.first:
                            sp.wait_ge(filled, 1)
                        if not head.early:
                            sp.wait_ge(s_done, plan.unit(head.back(1), 0))
                        for dst, src in ((KA[par][0:8, :], "kh"), (KA[par][LO0:LO0 + 8, :], "kl"),
                                         (KB[par][0:8, :], "kh"), (QA[par][0:8, :], "qh"),
                                         (QA[par][LO0:LO0 + 8, :], "qh"), (QB[par][0:8, :], "ql")):
                            sp.dma_start(dst.bitcast(F32), packed[src][head.h, :, :]).then_inc(kb_in[par], 16)

                prepare(static_head(0))
                load_wo(static_head(0), None)

                def period(head, nxt, last):
                    if last:
                        return
                    prepare(nxt)
                    load_wo(nxt, plan.job(head, ("Y", 1)) + 1 if not head.first else None)

                over_heads(sp, heads, period)

            @block.gpsimd
            def _(pool):
                def period(head, nxt, last):
                    for half in range(2):
                        acc = SUM[half]
                        for i in range(1, TILES):
                            u = half * TILES + i
                            kp = plan.tile_keys(i)
                            hi = HI[unit_slot(head, u)][0:kp, :].bitcast(F32)
                            pool.wait_ge(hi_done, plan.unit(head, u) + 1)
                            if i == 1:
                                if not head.first:
                                    pool.wait_ge(side_done, plan.post_job(head.back(1), half, "D", heads) + 1)
                                before = HI[unit_slot(head, u - 1)][0:kp, :].bitcast(F32)
                                pool.tensor_tensor(acc[0:kp, :], before, hi, ALU.add).then_inc(sum_done, 1)
                            else:
                                pool.wait_ge(sum_done, sums_before(head, half, i - 1))
                                pool.tensor_tensor(acc[0:kp, :], acc[0:kp, :], hi, ALU.add).then_inc(sum_done, 1)

                over_heads(pool, heads, period)

            @block.scalar
            def _(act):
                def side(head, n, job):
                    if job[0] not in "QKV":
                        return
                    act.wait_ge(side_done, n + 1)
                    ps = SIDE[side_bank(head, n, job)]
                    par = head.par
                    if job[0] == "Q":
                        act.activation(QA[par][:, job[1] * HALF:(job[1] + 1) * HALF], ps[:], ACT.Copy,
                                       scale=scale).then_inc(side_act, 1)
                    elif job[0] == "K":
                        m = plan.chunk_keys(job[1])
                        act.activation(KA[par][:, job[1] * CHUNK:job[1] * CHUNK + m], ps[:, 0:m], ACT.Copy)\
                           .then_inc(side_act, 1)
                    else:
                        if not head.early:
                            act.wait_ge(pv_done, plan.unit(head.back(1), 0))
                        last = None
                        for rows, t0, t1 in v_parts(job[1]):
                            o = v_offset(job[1], t0)
                            src = ps[0:rows, o * E:(o + t1 - t0) * E]
                            last = act.activation(V[par][0:rows, t0:t1, E:2 * E],
                                                  src.rearrange("p (t e) -> p t e", e=E), ACT.Copy)
                        last.then_inc(side_act, 1)

                act.wait_ge(filled, 1)
                h0 = static_head(0)
                for n, job in enumerate(plan.prep):
                    side(h0, n, job)

                def period(head, nxt, last):
                    for u in range(UNITS):
                        half, i = divmod(u, TILES)
                        kp = plan.tile_keys(i)
                        g = plan.unit(head, u)
                        slot = unit_slot(head, u)
                        act.wait_ge(s_done, g + 1)
                        if not (head.first and u < SLOTS):
                            act.wait_ge(pv_done, g - SLOTS + 1)
                            b = u - SLOTS
                            if b < 0:
                                act.wait_ge(sum_done, sums_before(head.back(1), 1, b + TILES))
                            else:
                                act.wait_ge(sum_done, sums_before(head, b // TILES, b % TILES))
                        act.activation(HI[slot][0:kp, :], S[slot][0:kp, :], ACT.Exp).then_inc(hi_done, 1)
                        act.activation(S[slot][0:kp, :], S[slot][0:kp, :], ACT.Exp).then_inc(p_done, 1)
                        for n, job in plan.jobs_at(head, last, u):
                            side(nxt, n, job)

                over_heads(act, heads, period)

            @block.vector
            def _(dve):
                for i in range(2):
                    dve.memset(KB[i][LO0:P, :].bitcast(F32), 1.0)
                    dve.memset(QB[i][LO0:P, :].bitcast(F32), 0.0)
                    if packed is not None:
                        dve.memset(KA[i][:].bitcast(F32), 0.0)
                        dve.memset(KB[i][0:LO0, :].bitcast(F32), 0.0)
                        dve.memset(QA[i][:].bitcast(F32), 0.0)
                        dve.memset(QB[i][0:LO0, :].bitcast(F32), 0.0)
                        dve.memset(V[i][:, :, 0:2 * E].bitcast(F32), 0.0)
                    elif KW > keys:
                        dve.memset(KA[i][:, keys:KW].bitcast(F32), 0.0)
                        dve.memset(KB[i][0:LO0, keys:KW].bitcast(F32), 0.0)
                    dve.memset(V[i][:, :, 2 * E:VW].bitcast(F32), 1.0)
                dve.memset(ones[:], 1.0).then_inc(max_step, 1)
                dve.wait_ge(max_step, 1)
                dve.engine_nop().then_inc(filled, 1)
                dve.wait_ge(bias_in, 16)
                dve.tensor_tensor(X[:], X[:], BIAS[:].unsqueeze(1).broadcast_to([P, NT, D]), ALU.add)\
                   .then_inc(bias_added, 1)

                def side(head, n, job):
                    ps = SIDE[side_bank(head, n, job)]
                    kind = job[0]
                    par = head.par if head is not None else None
                    if kind in "QKV":
                        dve.wait_ge(side_done, n + 1)
                        dve.wait_ge(side_act, act_count(head, job))
                        if kind == "Q":
                            q = slice(job[1] * HALF, (job[1] + 1) * HALF)
                            dve.scalar_tensor_tensor(QB[par][0:E, q], ps[0:E, :], scale, QA[par][0:E, q].bitcast(F32),
                                                     ALU.mult, ALU.subtract).then_inc(side_free, 1)
                        elif kind == "K":
                            m = plan.chunk_keys(job[1])
                            k = slice(job[1] * CHUNK, job[1] * CHUNK + m)
                            dve.tensor_tensor(KA[par][LO0:P, k], ps[LO0:P, 0:m], KA[par][LO0:P, k].bitcast(F32),
                                              ALU.subtract).then_inc(side_free, 1)
                        else:
                            last = None
                            for rows, t0, t1 in v_parts(job[1]):
                                o = v_offset(job[1], t0)
                                last = dve.tensor_tensor(
                                    V[par][0:rows, t0:t1, 0:E],
                                    ps[0:rows, o * E:(o + t1 - t0) * E].rearrange("p (t e) -> p t e", e=E),
                                    V[par][0:rows, t0:t1, E:2 * E].bitcast(F32), ALU.subtract)
                            last.then_inc(side_free, 1)
                    elif kind == "X":
                        if packed is not None and job[1:] == (0, 0):
                            if not head.early:
                                dve.wait_ge(pv_done, plan.unit(head.back(1), 0))
                            dve.tensor_copy(V[par][:, :, 0:8], VL[:, :, bass.ds(head.h * 8, 8)].bitcast(F32))
                            dve.tensor_copy(V[par][:, :, E:E + 8], VH[:, :, bass.ds(head.h * 8, 8)].bitcast(F32))
                        dve.wait_ge(side_done, n + 1)
                        dve.tensor_reduce(MX[:, job[1], job[2]:job[2] + 1], ps[:, 0:plan.chunk_keys(job[2])],
                                          AX.X, ALU.max).then_inc(side_free, 1)
                    elif kind == "M":
                        if job[1] == 0:
                            dve.wait_ge(side_free, n)
                            dve.tensor_reduce(NEGMAX[:], MX[:], AX.X, ALU.max, negate=True).then_inc(max_step, 1)
                            dve.wait_ge(max_step, 2 * head.h + 2)
                            dve.tensor_copy(SHIFT[:], NEGMAX[:]).then_inc(max_step, 1)
                        dve.wait_ge(side_done, n + 1)
                        q = slice(job[1] * HALF, (job[1] + 1) * HALF)
                        dve.tensor_copy(QB[par][LO0:LO0 + 1, q], ps[0:1, :]).then_inc(side_free, 1)
                    elif kind == "D":
                        dve.wait_ge(side_done, n + 1)
                        dve.reciprocal(RDEN[:], ps[:, 0:HALF // P]).then_inc(side_free, 1)
                    elif kind == "Y":
                        dve.wait_ge(side_done, n + 1)
                        dve.wait_ge(side_free, n)
                        dve.wait_ge(bias_added, 1)
                        last = None
                        for t in range(HALF // P):
                            xt = X[:, job[1] * (HALF // P) + t, :]
                            last = dve.scalar_tensor_tensor(xt, ps[:, t * D:(t + 1) * D], RDEN[:, t:t + 1], xt,
                                                            ALU.mult, ALU.add)
                        last.then_inc(side_free, 1)

                def take_output(head, half):
                    dve.wait_ge(pv_done, plan.unit(head, (half + 1) * TILES))
                    before = 3 * (2 * head.h + half)
                    dve.tensor_copy(OT[:], OA[:]).then_inc(evac, 1)
                    dve.tensor_copy(LOSUM[LO0:LO0 + 1, :], OB[LO0:LO0 + 1, :]).then_inc(evac, 1)
                    dve.wait_ge(evac, before + 1)
                    dve.tensor_tensor(OT[LO0:P, :], OB[0:E, :], OT[LO0:P, :], ALU.add).then_inc(evac, 1)

                def low_part(head, u):
                    kp = plan.tile_keys(u % TILES)
                    slot = unit_slot(head, u)
                    g = plan.unit(head, u)
                    dve.wait_ge(p_done, g + 1)
                    if not (head.first and u < SLOTS):
                        dve.wait_ge(pv_done, g - SLOTS + 1)
                    dve.tensor_tensor(LO[slot][0:kp, :], S[slot][0:kp, :], HI[slot][0:kp, :].bitcast(F32),
                                      ALU.subtract).then_inc(lo_done, 1)

                h0 = static_head(0)
                for n, job in enumerate(plan.prep):
                    side(h0, n, job)

                def period(head, nxt, last):
                    for u in range(UNITS):
                        if u == EVAC_STEP and not head.first:
                            take_output(head.back(1), 1)
                        if u == TILES + EVAC_STEP:
                            take_output(head, 0)
                        for n, job in plan.jobs_at(head, last, u):
                            side(nxt, n, job)
                        if u >= 1:
                            low_part(head, u - 1)
                        elif not head.first:
                            low_part(head.back(1), UNITS - 1)

                over_heads(dve, heads, period)
                end = static_head(heads - 1)
                low_part(end, UNITS - 1)
                take_output(end, 1)
                for kind in "DY":
                    side(None, plan.post_job(end, 1, kind, heads), (kind, 1))

            @block.tensor
            def _(pe):
                pe.wait_ge(filled, 1)

                def side(head, done, n, job):
                    ps = SIDE[side_bank(head, n, job)]
                    kind = job[0]
                    par = head.par if head is not None else None
                    if not isinstance(n, int) or n >= 2:
                        pe.wait_ge(side_free, n - 1)
                    if kind == "Q":
                        pe.wait_ge(w_in, 48 * (head.h + 1))
                        last = pe.matmul(ps[:], WQ[:], XT[:, job[1] * HALF:(job[1] + 1) * HALF], start=True, stop=True)
                    elif kind in "KV":
                        c = job[1]
                        m = plan.chunk_keys(c)
                        if ctx_dram is not None:
                            slot = ctx_slot(head, c)
                            pe.wait_ge(ctx_in[slot], ctx_count(head, c))
                            src = CTX[slot][0:C, 0:m]
                        else:
                            src = XT[:, c * CHUNK:c * CHUNK + m]
                        if kind == "K":
                            last = pe.matmul(ps[:, 0:m], WK[0:C, :], src, start=True, stop=True)
                        else:
                            for j in range(-(-m // P)):
                                rows = min(P, m - j * P)
                                last = pe.matmul(ps[0:rows, j * E:(j + 1) * E], src[:, j * P:j * P + rows],
                                                 WV[0:C, :], start=True, stop=True)
                    elif kind == "X":
                        t, c = job[1:]
                        m = plan.chunk_keys(c)
                        if packed is None:
                            pe.wait_ge(side_free, plan.prep_job(head, ("K", c)) + 1)
                        else:
                            pe.wait_ge(kb_in[par], 16 * KB_DMAS * (head.hp + 1))
                        last = pe.matmul(ps[:, 0:m], QA[par][:, t * P:(t + 1) * P],
                                         KA[par][:, c * CHUNK:c * CHUNK + m], start=True, stop=True)
                    elif kind == "M":
                        pe.wait_ge(max_step, 2 * head.h + 3)
                        for j in range(HALF // P):
                            t = job[1] * (HALF // P) + j
                            last = pe.matmul(ps[0:1, j * P:(j + 1) * P], SHIFT[:, t:t + 1].bitcast(F32), ident[:],
                                             start=True, stop=True)
                    elif kind == "D":
                        pe.wait_ge(evac, 3 * (2 * done.h + job[1] + 1))
                        pe.wait_ge(sum_done, (2 * done.h + job[1] + 1) * (TILES - 1))
                        for t in range(HALF // P):
                            q = slice(t * P, (t + 1) * P)
                            pe.matmul(ps[:, t:t + 1], SUM[job[1]][:, q], ones[:, 0:1], start=True, stop=False)
                            last = pe.matmul(ps[:, t:t + 1], LOSUM[LO0:LO0 + 1, q], ones[LO0:LO0 + 1, 0:1],
                                             start=False, stop=True)
                    elif kind == "Y":
                        pe.wait_ge(wo_in[done.par], 16 * (done.hp + 1))
                        for t in range(HALF // P):
                            last = pe.matmul(ps[:, t * D:(t + 1) * D], OT[:, t * P:(t + 1) * P], WO[done.par][:],
                                             start=True, stop=True)
                    last.then_inc(side_done, 1)

                def scores(head, u):
                    half, i = divmod(u, TILES)
                    slot = unit_slot(head, u)
                    g = plan.unit(head, u)
                    if u == 0:
                        prep_done = plan.prep_job(head, ("M", 1)) + 1
                        pe.wait_ge(side_free, prep_done)
                        pe.wait_ge(kb_in[head.par], 16 * KB_DMAS * (head.hp + 1))
                    if not (head.first and u < SLOTS):
                        pe.wait_ge(lo_done, g - SLOTS + 1)
                    k = slice(i * P, (i + 1) * P)
                    q = slice(half * HALF, (half + 1) * HALF)
                    pe.matmul(S[slot][:], KA[head.par][:, k], QA[head.par][:, q], start=True, stop=False)
                    pe.matmul(S[slot][:], KB[head.par][:, k], QB[head.par][:, q], start=False, stop=True)\
                      .then_inc(s_done, 1)

                def product(head, u):
                    half, i = divmod(u, TILES)
                    kp = plan.tile_keys(i)
                    slot = unit_slot(head, u)
                    g = plan.unit(head, u)
                    ends = dict(start=i == 0, stop=i == TILES - 1)
                    if i == 0 and not (head.first and half == 0):
                        pe.wait_ge(evac, 3 * (2 * head.h + half))
                    pe.wait_ge(lo_done, g + 1)
                    pe.matmul(OA[:], V[head.par][0:kp, i, 0:2 * E], HI[slot][0:kp, :], **ends)
                    pe.matmul(OB[0:E + 1, :], V[head.par][0:kp, i, E:VW], LO[slot][0:kp, :], **ends)\
                      .then_inc(pv_done, 1)

                h0 = static_head(0)
                for n, job in enumerate(plan.prep):
                    side(h0, None, n, job)

                def period(head, nxt, last):
                    for u in range(UNITS):
                        scores(head, u)
                        for n, job in plan.jobs_at(head, last, u):
                            side(nxt, head if job[1] == 0 or job[0] not in "DY" else head.back(1), n, job)
                        if u >= LAG:
                            product(head, u - LAG)
                        elif not head.first:
                            product(head.back(1), UNITS + u - LAG)

                over_heads(pe, heads, period)
                end = static_head(heads - 1)
                for u in range(UNITS - LAG, UNITS):
                    product(end, u)
                for kind in "DY":
                    side(None, end, plan.post_job(end, 1, kind, heads), (kind, 1))


class NormSemaphores:

    def __init__(self, nc, held):
        self.loaded, self.stats, self.var_in, self.rstd, self.normed, self.turned, self.copied = [
            held.enter_context(nc.semaphore(f"norm_{n}"))
            for n in ("loaded", "stats", "var_in", "rstd", "normed", "turned", "copied")]
        self.norms = 0


def layer_norm(nc, sems, name, eps, src, XH, XT, ident, load=None):
    with ExitStack() as ctx:
        def sb(n, shape, dt=F32):
            return ctx.enter_context(nc.sbuf_tensor(f"{name}_{n}", shape, dt))

        STATS = sb("STATS", [P, NT, 6])
        MV = sb("MV", [P, NT, 2])
        VE = sb("VE", [P, NT])
        POWER = sb("POWER", [P, NT])
        RSTD = sb("RSTD", [P, NT])
        T = [ctx.enter_context(nc.psum_tensor(f"{name}_T{i}", [P, 512], F32)) for i in range(2)]
        k = sems.norms
        sems.norms += 1

        with nc.Block() as block:

            if load is not None:
                @block.sync
                def _(sp):
                    for dst, dram in load:
                        sp.dma_start(dst, dram).then_inc(sems.loaded, 16)

            @block.vector
            def _(dve):
                if load is not None:
                    dve.wait_ge(sems.loaded, 16 * len(load))
                for t in range(NT):
                    dve.bn_stats(STATS[:, t, :], src[:, t, :]).then_inc(sems.stats, 1)
                for t in range(NT):
                    dve.wait_ge(sems.stats, 2 * NT * k + t + 1)
                    dve.bn_aggr(MV[:, t, :], STATS[:, t, :]).then_inc(sems.stats, 1)
                dve.wait_ge(sems.stats, 2 * NT * (k + 1))
                dve.memset(POWER[:], -0.5)
                dve.tensor_scalar(VE[:], MV[:, :, 1], eps, None, ALU.add).then_inc(sems.var_in, 1)
                dve.wait_ge(sems.rstd, k + 1)
                for t in range(NT):
                    dve.tensor_scalar(XH[:, t, :], src[:, t, :], MV[:, t, 0:1], RSTD[:, t:t + 1],
                                      ALU.subtract, ALU.mult).then_inc(sems.normed, 1)
                dve.wait_ge(sems.turned, 2 * k + 1)
                dve.tensor_copy(XT[:, 0:512], T[0][:]).then_inc(sems.copied, 1)

            @block.gpsimd
            def _(pool):
                pool.wait_ge(sems.var_in, k + 1)
                pool.tensor_tensor(RSTD[:], VE[:], POWER[:], ALU.pow).then_inc(sems.rstd, 1)

            @block.tensor
            def _(pe):
                for t in range(NT):
                    pe.wait_ge(sems.normed, NT * k + t + 1)
                    last = pe.transpose(T[t // 4][:, t % 4 * P:(t % 4 + 1) * P], XH[:, t, :], ident[:])
                    if t % 4 == 3:
                        last.then_inc(sems.turned, 1)

            @block.scalar
            def _(act):
                act.wait_ge(sems.turned, 2 * k + 2)
                act.activation(XT[:, 512:1024], T[1][:], ACT.Copy).then_inc(sems.copied, 1)


def rotary(nc, held, name, XT, w_dram, tables, scratch, VH, VL, scale):
    with ExitStack() as ctx:
        def sb(n, shape, dt=F32):
            return ctx.enter_context(nc.sbuf_tensor(f"{name}_{n}", shape, dt))

        def sem(n):
            return held.enter_context(nc.semaphore(f"{name}_{n}"))

        W = [sb(f"W{i}", [P, P]) for i in range(4)]
        COS, SIN = sb("COS", [P, N]), sb("SIN", [P, N])
        COSV, SINV = sb("COSV", [P, NT, P]), sb("SINV", [P, NT, P])
        A = [sb(f"A{i}", [P, N]) for i in range(3)]
        B = [sb(f"B{i}", [P, N]) for i in range(3)]
        PARTS = {n: sb(n, [P, N], F32R) for n in ("qh", "ql", "kh", "kl")}
        BANK = [ctx.enter_context(nc.psum_tensor(f"{name}_BANK{i}", [P, 512], F32)) for i in range(8)]
        w_in, projected, step, out = sem("w_in"), sem("projected"), sem("step"), sem("out")

        with nc.Block() as block:

            @block.sync
            def _(sp):
                for i in range(4):
                    sp.dma_start(W[i][:], w_dram[i]).then_inc(w_in, 16)
                sp.dma_start(COS[:], tables[0]).then_inc(w_in, 16)
                sp.dma_start(SIN[:], tables[1]).then_inc(w_in, 16)
                sp.dma_start(COSV[:], tables[2].rearrange("(t p) d -> p t d", p=P)).then_inc(w_in, 16)
                sp.dma_start(SINV[:], tables[3].rearrange("(t p) d -> p t d", p=P)).then_inc(w_in, 16)
                sp.wait_ge(step, 20)
                for n in ("qh", "ql", "kh", "kl"):
                    sp.dma_start(scratch[n].rearrange("h d n -> (h d) n"), PARTS[n][:].bitcast(F32)).then_inc(out, 16)
                sp.wait_ge(out, 64)

            @block.tensor
            def _(pe):
                pe.wait_ge(w_in, 128)
                for i in range(4):
                    for half in range(2):
                        pe.matmul(BANK[2 * i + half][:], W[i][:], XT[:, half * 512:(half + 1) * 512],
                                  start=True, stop=True).then_inc(projected, 1)
                pe.wait_ge(step, 4)
                for t in range(NT):
                    for i in range(2):
                        pe.matmul(BANK[2 * i + t // 4][:, t % 4 * P:(t % 4 + 1) * P], XT[:, t * P:(t + 1) * P],
                                  W[2 + i][:], start=True, stop=True).then_inc(projected, 1)

            @block.vector
            def _(dve):
                count = 0

                def turn(b0, a, b, cos, sin):
                    for half in range(2):
                        h = slice(half * 512, (half + 1) * 512)
                        dve.tensor_tensor(a[:, h], BANK[b0 + half][:], cos[:, h], ALU.mult).then_inc(step, 1)
                        dve.tensor_tensor(b[:, h], BANK[b0 + 2 + half][:], sin[:, h], ALU.mult).then_inc(step, 1)

                flat = [t[:].rearrange("p t d -> p (t d)") for t in (COSV, SINV)]
                dve.wait_ge(w_in, 128)
                dve.wait_ge(projected, 8)
                turn(0, A[0], B[0], COS[:], SIN[:])
                turn(4, A[1], B[1], COS[:], SIN[:])
                dve.wait_ge(projected, 8 + 2 * NT)
                turn(0, A[2], B[2], flat[0], flat[1])
                dve.wait_ge(step, 12)
                for i in range(3):
                    dve.tensor_tensor(A[i][:], A[i][:], B[i][:], ALU.add).then_inc(step, 1)
                dve.wait_ge(step, 15)
                dve.tensor_scalar(B[0][:], A[0][:], scale, None, ALU.mult).then_inc(step, 1)
                dve.wait_ge(step, 16)
                hi = (PARTS["qh"][:], PARTS["kh"][:], VH[:].rearrange("p t d -> p (t d)"))
                lo = (PARTS["ql"][:], PARTS["kl"][:], VL[:].rearrange("p t d -> p (t d)"))
                x = (B[0], A[1], A[2])
                for i in range(3):
                    last = dve.tensor_copy(hi[i], x[i][:])
                last.then_inc(step, 1)
                dve.wait_ge(step, 17)
                for i in range(3):
                    dve.tensor_tensor(lo[i], x[i][:], hi[i].bitcast(F32), ALU.subtract).then_inc(step, 1)


def experts(nc, held, name, count, gated, X, XH, XT, ident, dram, func, normed):
    XT_in = normed if normed is not None else XT
    F = 512
    KF = F // P
    with ExitStack() as ctx:
        def sb(n, shape, dt=F32):
            return ctx.enter_context(nc.sbuf_tensor(f"{name}_{n}", shape, dt))

        def sem(n):
            return held.enter_context(nc.semaphore(f"{name}_{n}"))

        G = gated
        GW = sb("GW", [P, G])
        GB = sb("GB", [P, G])
        B2 = sb("B2", [16, D])
        W1 = [sb(f"W1{i}", [P, F]) for i in range(2)]
        W2 = [sb(f"W2{i}", [P, KF, D]) for i in range(2)]
        B1 = [sb(f"B1{i}", [P, KF]) for i in range(2)]
        AFF = [sb(f"AFF{i}", [P, 2]) for i in range(2)]
        XE = [sb(f"XE{i}", [P, N]) for i in range(2)] if normed is not None else [XT, XT]
        H = [sb(f"H{i}", [P, KF, N]) for i in range(2)]
        WE = [sb(f"WE{i}", [P, NT]) for i in range(2)]
        ACC = sb("ACC", [P, NT, D])
        WT = sb("WT", [16, N])
        R = {n: sb(n, [P, NT, G]) for n in ("score", "prob", "eq", "one1", "one2", "rest", "tmp")}
        REV = sb("REV", [P, NT, G])
        WALL = sb("WALL", [P, NT, count])
        C = {n: sb(n, [P, NT]) for n in ("m", "neg", "den", "rden", "v1", "v2", "pos", "sum", "e", "w1", "w2")}
        UP = [ctx.enter_context(nc.psum_tensor(f"{name}_UP{i}", [P, 512], F32)) for i in range(4)]
        DN = [ctx.enter_context(nc.psum_tensor(f"{name}_DN{i}", [P, 512], F32)) for i in range(4)]
        const_in, logits, r, exp_done, turned, wt, b2_done, acc0 = [
            sem(n) for n in ("const_in", "logits", "r", "exp_done", "turned", "wt", "b2_done", "acc0")]
        w_in = [sem(f"w_in{i}") for i in range(2)]
        up_done, h_done, dn_done, acc_done, xe_done, x_done = [
            sem(n) for n in ("up_done", "h_done", "dn_done", "acc_done", "xe_done", "x_done")]
        PER_W = 16 * (4 if normed is not None else 3)

        def loop(eng, body):
            with eng.Fori(0, (count - 1) // 2) as it:
                body(2 * it, 0, it)
                body(2 * it + 1, 1, it)
            for e in range((count - 1) // 2 * 2, count - 1):
                body(e, e % 2, e // 2)

        with nc.Block() as block:

            @block.sync
            def _(sp):
                sp.dma_start(GW[:], dram["gate"]).then_inc(const_in, 16)
                if dram["gate_b"] is not None:
                    sp.dma_start(GB[:], dram["gate_b"].partition_broadcast(P)).then_inc(const_in, 16)
                sp.dma_start(B2[0:count, :], dram["b2"]).then_inc(const_in, 16)

                def load(e, par):
                    sp.dma_start(W1[par][:], dram["w1"][e, :, :]).then_inc(w_in[par], 16)
                    sp.dma_start(W2[par][:], dram["w2"][e, :, :, :]).then_inc(w_in[par], 16)
                    sp.dma_start(B1[par][:], dram["b1"][e, :, :]).then_inc(w_in[par], 16)
                    if normed is not None:
                        sp.dma_start(AFF[par][:], dram["affine"][e, :, :]).then_inc(w_in[par], 16)

                load(0, 0)
                load(1, 1)

                def body(e, par, ep):
                    sp.wait_ge(dn_done, 2 * e + 2)
                    load(e + 2, par)

                with sp.Fori(0, (count - 2) // 2) as it:
                    body(2 * it, 0, it)
                    body(2 * it + 1, 1, it)
                for e in range((count - 2) // 2 * 2, count - 2):
                    body(e, e % 2, e // 2)

            @block.tensor
            def _(pe):
                pe.wait_ge(const_in, 16 * (2 + (dram["gate_b"] is not None)))
                for t in range(NT):
                    last = pe.matmul(UP[0][:, t * G:(t + 1) * G], XT[:, t * P:(t + 1) * P], GW[:], start=True, stop=True)
                last.then_inc(logits, 1)
                pe.wait_ge(wt, 1)
                for t in range(NT):
                    last = pe.transpose(UP[t // 4][0:count, t % 4 * P:(t % 4 + 1) * P], WALL[:, t, :], ident[:])
                last.then_inc(turned, 1)
                pe.wait_ge(wt, 3)
                for t in range(NT):
                    last = pe.matmul(DN[t // 4][:, t % 4 * D:(t % 4 + 1) * D], WT[0:count, t * P:(t + 1) * P],
                                     B2[0:count, :], start=True, stop=True)
                last.then_inc(b2_done, 1)
                pe.wait_ge(acc0, 1)

                def up(e, par, ep):
                    pe.wait_ge(w_in[par], PER_W * (ep + 1))
                    if normed is not None:
                        pe.wait_ge(xe_done, e + 1)
                    for k in range(KF):
                        for half in range(2):
                            j = 2 * k + half
                            if not (isinstance(e, int) and e == 0 and j < 4):
                                pe.wait_ge(h_done, 8 * e + j - 3)
                            pe.matmul(UP[j % 4][:], W1[par][:, k * P:(k + 1) * P],
                                      XE[par][:, half * 512:(half + 1) * 512], start=True, stop=True)\
                              .then_inc(up_done, 1)

                def down(e, par, ep):
                    pe.wait_ge(h_done, 8 * e + 8)
                    for g in range(2):
                        if not isinstance(e, int) or e >= 2:
                            pe.wait_ge(acc_done, 2 * e + g - 3 + 4)
                        for j in range(4):
                            t = 4 * g + j
                            for k in range(KF):
                                last = pe.matmul(DN[2 * par + g][:, j * D:(j + 1) * D], H[par][:, k, t * P:(t + 1) * P],
                                                 W2[par][:, k, :], start=k == 0, stop=k == KF - 1)
                        last.then_inc(dn_done, 1)

                up(0, 0, 0)

                def body(e, par, ep):
                    up(e + 1, 1 - par, ep + par)
                    down(e, par, ep)

                loop(pe, body)
                down(count - 1, (count - 1) % 2, (count - 1) // 2)

            @block.scalar
            def _(act):
                if normed is None:
                    act.wait_ge(r, 4)
                    act.activation(R["prob"][:], R["tmp"][:], ACT.Exp).then_inc(exp_done, 1)
                else:
                    act.wait_ge(r, 12)
                    act.activation(C["e"][:], C["neg"][:], ACT.Exp).then_inc(exp_done, 1)
                act.wait_ge(turned, 1)
                act.activation(WT[0:count, 512:1024], UP[1][0:count, :], ACT.Copy).then_inc(wt, 1)

                def hidden(e, par, ep):
                    for k in range(KF):
                        for half in range(2):
                            j = 2 * k + half
                            act.wait_ge(up_done, 8 * e + j + 1)
                            act.activation(H[par][:, k, half * 512:(half + 1) * 512], UP[j % 4][:], func,
                                           bias=B1[par][:, k:k + 1]).then_inc(h_done, 1)

                hidden(0, 0, 0)
                loop(act, lambda e, par, ep: hidden(e + 1, 1 - par, ep + par))

            @block.vector
            def _(dve):
                for e in range(G):
                    dve.memset(REV[:, :, e], float(G - e))
                dve.memset(WALL[:], 1.0).then_inc(r, 1)
                steps = 1

                def then(ins):
                    nonlocal steps
                    steps += 1
                    ins.then_inc(r, 1)
                    dve.wait_ge(r, steps)

                def wide(c):
                    return c[:].unsqueeze(2).broadcast_to([P, NT, G])

                def pick(src, one, value):
                    then(dve.tensor_reduce(value[:], src[:], AX.X, ALU.max))
                    then(dve.tensor_tensor(R["eq"][:], src[:], wide(value), ALU.is_equal))
                    then(dve.tensor_tensor(R["eq"][:], R["eq"][:], REV[:], ALU.mult))
                    then(dve.tensor_reduce(C["pos"][:], R["eq"][:], AX.X, ALU.max))
                    then(dve.tensor_tensor(one[:], R["eq"][:], wide(C["pos"]), ALU.is_equal))

                dve.wait_ge(r, 1)
                dve.wait_ge(logits, 1)
                lg = UP[0][:, 0:NT * G].rearrange("p (t e) -> p t e", e=G)
                if normed is None:
                    then(dve.tensor_tensor(R["score"][:], lg, GB[:].unsqueeze(1).broadcast_to([P, NT, G]), ALU.add))
                    then(dve.tensor_reduce(C["m"][:], R["score"][:], AX.X, ALU.max))
                    then(dve.tensor_tensor(R["tmp"][:], R["score"][:], wide(C["m"]), ALU.subtract))
                    dve.wait_ge(exp_done, 1)
                    then(dve.tensor_reduce(C["den"][:], R["prob"][:], AX.X, ALU.add))
                    then(dve.reciprocal(C["rden"][:], C["den"][:]))
                    then(dve.tensor_tensor(R["score"][:], R["prob"][:], wide(C["rden"]), ALU.mult))
                    pick(R["score"], R["one1"], C["v1"])
                    then(dve.scalar_tensor_tensor(R["rest"][:], R["one1"][:], -2.0, R["score"][:], ALU.mult, ALU.add))
                    pick(R["rest"], R["one2"], C["v2"])
                    then(dve.tensor_tensor(C["sum"][:], C["v1"][:], C["v2"][:], ALU.add))
                    then(dve.tensor_scalar(C["sum"][:], C["sum"][:], 1e-9, None, ALU.add))
                    then(dve.reciprocal(C["rden"][:], C["sum"][:]))
                    then(dve.tensor_tensor(C["w1"][:], C["v1"][:], C["rden"][:], ALU.mult))
                    then(dve.tensor_tensor(C["w2"][:], C["v2"][:], C["rden"][:], ALU.mult))
                else:
                    then(dve.tensor_copy(R["score"][:], lg))
                    pick(R["score"], R["one1"], C["v1"])
                    then(dve.scalar_tensor_tensor(R["rest"][:], R["one1"][:], -3e38, R["score"][:], ALU.mult, ALU.add))
                    then(dve.tensor_reduce(C["v2"][:], R["rest"][:], AX.X, ALU.max))
                    then(dve.tensor_tensor(R["eq"][:], R["rest"][:], wide(C["v2"]), ALU.is_equal))
                    then(dve.tensor_tensor(R["eq"][:], R["eq"][:], REV[:], ALU.mult))
                    then(dve.tensor_tensor(C["neg"][:], C["v2"][:], C["v1"][:], ALU.subtract))
                    assert steps == 12
                    then(dve.tensor_reduce(C["pos"][:], R["eq"][:], AX.X, ALU.max))
                    then(dve.tensor_tensor(R["one2"][:], R["eq"][:], wide(C["pos"]), ALU.is_equal))
                    dve.wait_ge(exp_done, 1)
                    then(dve.tensor_scalar(C["den"][:], C["e"][:], 1.0, None, ALU.add))
                    then(dve.reciprocal(C["w1"][:], C["den"][:]))
                    then(dve.tensor_tensor(C["w2"][:], C["e"][:], C["w1"][:], ALU.mult))
                    then(dve.tensor_tensor(C["sum"][:], C["w1"][:], C["w2"][:], ALU.add))
                then(dve.tensor_tensor(R["one1"][:], R["one1"][:], wide(C["w1"]), ALU.mult))
                then(dve.tensor_tensor(R["one2"][:], R["one2"][:], wide(C["w2"]), ALU.mult))
                dve.tensor_tensor(WALL[:, :, 0:G], R["one1"][:], R["one2"][:], ALU.add).then_inc(wt, 1)
                dve.wait_ge(turned, 1)
                dve.tensor_copy(WT[0:count, 0:512], UP[0][0:count, :]).then_inc(wt, 1)
                dve.wait_ge(b2_done, 1)
                for g in range(2):
                    dve.tensor_copy(ACC[:, 4 * g:4 * g + 4, :],
                                    DN[g][:].rearrange("p (t d) -> p t d", d=D)).then_inc(acc_done, 1)
                dve.wait_ge(acc_done, 2)
                if normed is None:
                    dve.tensor_tensor(ACC[:], ACC[:], XH[:], ALU.add).then_inc(acc_done, 1)
                else:
                    for t in range(NT):
                        last = dve.scalar_tensor_tensor(ACC[:, t, :], XH[:, t, :], C["sum"][:, t:t + 1], ACC[:, t, :],
                                                        ALU.mult, ALU.add)
                    last.then_inc(acc_done, 1)
                dve.wait_ge(acc_done, 3)
                dve.tensor_tensor(ACC[:], ACC[:], X[:], ALU.add).then_inc(acc_done, 1)
                dve.wait_ge(acc_done, 4)
                dve.engine_nop().then_inc(acc0, 1)

                def affine(e, par, ep):
                    dve.wait_ge(w_in[par], PER_W * (ep + 1))
                    if not isinstance(e, int) or e >= 2:
                        dve.wait_ge(up_done, 8 * e - 7)
                    dve.tensor_scalar(XE[par][:], XT_in[:], AFF[par][:, 0:1], AFF[par][:, 1:2], ALU.mult, ALU.add)\
                       .then_inc(xe_done, 1)

                def add(e, par, ep):
                    dve.wait_ge(acc_done, 2 * e + 4)
                    dve.tensor_copy(WE[par][:], WALL[:, :, bass.ds(e, 1)].rearrange("p t e -> p (t e)"))\
                       .then_inc(x_done, 1)
                    dve.wait_ge(x_done, e + 1)
                    for g in range(2):
                        dve.wait_ge(dn_done, 2 * e + g + 1)
                        for j in range(4):
                            t = 4 * g + j
                            last = dve.scalar_tensor_tensor(ACC[:, t, :], DN[2 * par + g][:, j * D:(j + 1) * D],
                                                            WE[par][:, t:t + 1], ACC[:, t, :], ALU.mult, ALU.add)
                        last.then_inc(acc_done, 1)

                if normed is not None:
                    affine(0, 0, 0)

                def body(e, par, ep):
                    if normed is not None:
                        affine(e + 1, 1 - par, ep + par)
                    add(e, par, ep)

                loop(dve, body)
                add(count - 1, (count - 1) % 2, (count - 1) // 2)
                dve.wait_ge(acc_done, 2 * count + 4)
                dve.tensor_copy(X[:], ACC[:]).then_inc(x_done, 1)


def store(nc, X, out):
    with ExitStack() as ctx:
        stored = ctx.enter_context(nc.semaphore("stored"))
        with nc.Block() as block:
            @block.sync
            def _(sp):
                sp.dma_start(out.rearrange("b (t p) d -> p (b t) d", p=P), X[:]).then_inc(stored, 16)
                sp.wait_ge(stored, 16)


def build(nc, a, out, stages=None):
    with ExitStack() as held, ExitStack() as ctx:
        norms = NormSemaphores(nc, held)

        def sb(n, shape, dt=F32):
            return ctx.enter_context(nc.sbuf_tensor(n, shape, dt))

        X = sb("X", [P, NT, D])
        XH = sb("XH", [P, NT, D])
        XT = sb("XT", [P, N])
        ident = sb("ident", [P, P])
        x_dram = a["x"].rearrange("b (t p) d -> p (b t) d", p=P)
        on = (lambda s: stages is None or s in stages)
        layer_norm(nc, norms, "ln0", 1e-5, X, XH, XT, ident, load=[(X[:], x_dram), (ident[:], a["ident"])])
        if on("a0"):
            attention(nc, held, "a0", 16, N, X, XT, ident, [a[f"L0_attn_{n}"] for n in ("Wq", "Wk", "Wv", "Wp")],
                      a["L0_attn_bp"])
        if on("c0"):
            layer_norm(nc, norms, "ln1", 1e-5, X, XH, XT, ident)
            attention(nc, held, "c0", 16, a["ctx"].shape[1], X, XT, ident,
                      [a[f"L0_xattn_{n}"] for n in ("Wq", "Wk", "Wv", "Wo")], a["L0_xattn_bo"], ctx_dram=a["ctx"])
        if on("f0"):
            layer_norm(nc, norms, "ln2", 1e-5, X, XH, XT, ident)
            experts(nc, held, "f0", 9, 8, X, XH, XT, ident,
                    dict(gate=a["L0_ffn_gate_w"], gate_b=a["L0_ffn_gate_b"], w1=a["L0_w1"], b1=a["L0_b1"],
                         w2=a["L0_w2"], b2=a["L0_b2"]), ACT.Gelu_apprx_tanh, None)
        if on("a1"):
            layer_norm(nc, norms, "ln3", 1e-5, X, XH, XT, ident)
            with nc.sbuf_tensor("VH", [P, NT, P], F32R) as VH, nc.sbuf_tensor("VL", [P, NT, P], F32R) as VL:
                scratch = {n: nc.dram_tensor(f"scratch_{n}", (16, 8, N), F32, kind="Internal").ap()
                           for n in ("qh", "ql", "kh", "kl")}
                rotary(nc, held, "rot", XT, [a[n] for n in ("L1_attn_Wq", "L1_attn_Wq_turned", "L1_attn_Wkv",
                                                      "L1_attn_Wkv_turned")],
                       [a[n] for n in ("cos", "sin", "cos_t", "sin_t")], scratch, VH, VL, float(np.float32(8 ** -0.5)))
                attention(nc, held, "a1", 16, N, X, XT, ident, [None, None, None, a["L1_attn_Wout"]], a["L1_attn_bout"],
                          packed=dict(scratch, vh=VH, vl=VL))
        if on("c1"):
            layer_norm(nc, norms, "ln4", 1e-5, X, XH, XT, ident)
            attention(nc, held, "c1", 8, a["ctx"].shape[1], X, XT, ident,
                      [a[f"L1_xattn_{n}"] for n in ("Wq", "Wk", "Wv", "Wo")], a["L1_xattn_bo"], ctx_dram=a["ctx"])
        if on("f1"):
            layer_norm(nc, norms, "ln5", 1e-5, X, XH, XT, ident)
            XH2, XT2 = sb("XH2", [P, NT, D]), sb("XT2", [P, N])
            layer_norm(nc, norms, "ln6", 1e-6, XH, XH2, XT2, ident)
            experts(nc, held, "f1", 8, 8, X, XH, XT, ident,
                    dict(gate=a["L1_ffn_Wg"], gate_b=None, w1=a["L1_w1"], b1=a["L1_b1"], w2=a["L1_w2"],
                         b2=a["L1_b2"], affine=a["L1_affine"]), ACT.Relu, XT2)
        store(nc, X, out)


def lay_out(x):
    f = np.float32
    x = {k: np.asarray(v) for k, v in x.items()}
    o = {"x": x["x"], "ctx": x["ctx_768"][0].T, "ident": np.eye(P, dtype=f)}

    def twice(w):
        return np.concatenate([w, w], axis=2)

    def split(w, h):
        return w.reshape(w.shape[0], h, -1).transpose(1, 0, 2)

    def rows_twice(w):
        out = np.zeros((w.shape[0], 2, E, w.shape[2]), f)
        out[:, :, :w.shape[1]] = w[:, None]
        return out.reshape(w.shape[0], 2 * E, w.shape[2])

    o["L0_attn_Wq"], o["L0_attn_Wk"], o["L0_attn_Wv"] = twice(x["L0_attn_Wq"]), twice(x["L0_attn_Wk"]), x["L0_attn_Wv"]
    o["L0_attn_Wp"] = rows_twice(x["L0_attn_Wp"].reshape(E, 16, D).transpose(1, 0, 2))
    for n, h in (("L0", 16), ("L1", 8)):
        for m in ("Wq", "Wk"):
            o[f"{n}_xattn_{m}"] = twice(split(x[f"{n}_xattn_{m}"], h))
        o[f"{n}_xattn_Wv"] = split(x[f"{n}_xattn_Wv"], h)
        o[f"{n}_xattn_Wo"] = rows_twice(x[f"{n}_xattn_Wo"].reshape(h, E, D))
        o[f"{n}_xattn_bo"] = x[f"{n}_xattn_bo"]
    o["L0_attn_bp"] = x["L0_attn_bp"]
    o["L0_ffn_gate_w"], o["L0_ffn_gate_b"] = x["L0_ffn_gate_w"], x["L0_ffn_gate_b"]

    def by_rows(b):
        return b.reshape(b.shape[0], -1, P).transpose(0, 2, 1)

    def by_row_tiles(w):
        return w.reshape(w.shape[0], -1, P, D).transpose(0, 2, 1, 3)

    o["L0_w1"] = np.concatenate([x["L0_ffn_ew1"], x["L0_ffn_sh_w1"][None]])
    o["L0_b1"] = by_rows(np.concatenate([x["L0_ffn_eb1"], x["L0_ffn_sh_b1"][None]]))
    o["L0_w2"] = by_row_tiles(np.concatenate([x["L0_ffn_ew2"], x["L0_ffn_sh_w2"][None]]))
    o["L0_b2"] = np.concatenate([x["L0_ffn_eb2"], x["L0_ffn_sh_b2"][None]])
    perm = np.arange(P).reshape(16, 2, 4)[:, ::-1].reshape(P)
    for n in ("Wq", "Wkv"):
        o[f"L1_attn_{n}"], o[f"L1_attn_{n}_turned"] = x[f"L1_attn_{n}"], x[f"L1_attn_{n}"][:, perm]
    o["L1_attn_Wout"] = rows_twice(x["L1_attn_Wout"].reshape(16, 8, D))
    o["L1_attn_bout"] = x["L1_attn_bout"]
    freq = f(1.0) / f(10000.0) ** (np.arange(0, 8, 2, dtype=f) / f(8))
    angle = np.outer(np.arange(N, dtype=f), freq).astype(f)
    cos = np.tile(np.cos(angle), (1, 2 * 16)).astype(f)
    sin = np.tile(np.concatenate([-np.sin(angle), np.sin(angle)], axis=1), (1, 16)).astype(f)
    o["cos_t"], o["sin_t"], o["cos"], o["sin"] = cos, sin, cos.T, sin.T
    o["L1_ffn_Wg"] = x["L1_ffn_Wg"]
    o["L1_w1"], o["L1_b1"] = x["L1_ffn_W1"], by_rows(x["L1_ffn_b1"])
    o["L1_w2"], o["L1_b2"] = by_row_tiles(x["L1_ffn_W2"]), x["L1_ffn_b2"]
    o["L1_affine"] = np.stack([x["L1_ffn_gamma"], x["L1_ffn_beta"]], axis=2)
    return {k: np.ascontiguousarray(v) for k, v in o.items()}


def kernel(**inputs):
    import concourse.bacc as bacc
    from concourse.bass_utils import run_bass_kernel_spmd

    arrays = lay_out(inputs)
    nc = bacc.Bacc("TRN2", target_bir_lowering=False, num_devices=1, dynamic_dma_scratch_size=1024)
    aps = {n: nc.dram_tensor(f"in_{n}", v.shape, mybir.dt.from_np(v.dtype), kind="ExternalInput").ap()
           for n, v in arrays.items()}
    out = nc.dram_tensor("out", (1, N, D), F32, kind="ExternalOutput").ap()
    build(nc, aps, out)
    r = run_bass_kernel_spmd(nc, [{f"in_{n}": v for n, v in arrays.items()}], core_ids=[0])
    return r.results[0]["out"]
```

```python
from contextlib import ExitStack

import numpy as np

import concourse.bass as bass
from concourse import mybir

F32 = mybir.dt.float32
F32R = mybir.dt.float32r
ALU = mybir.AluOpType
ACT = mybir.ActivationFunctionType
AX = mybir.AxisListType

P = 128
N = 1024
D = 128
NT = N // P
HALF = 512
CHUNK = 512
E = 64
LO0 = 64
VW = 2 * E + 1
SLOTS = 4
SUM_ROW = 32
LOW_LAG = 1


class Head:

    def __init__(self, h, par, hp):
        self.h, self.par, self.hp = h, par, hp
        self.first = isinstance(h, int) and h == 0
        self.early = isinstance(h, int) and h < 2

    def back(self, n):
        if n == 2:
            return Head(self.h - 2, self.par, self.hp - 1)
        return Head(self.h - 1, 1 - self.par, self.hp - (1 - self.par))


def static_head(h):
    return Head(h, h % 2, h // 2)


def over_heads(eng, heads, period):
    period(static_head(0), static_head(1), False)
    with eng.Fori(0, (heads - 2) // 2) as it:
        odd, even, odd2 = Head(1 + 2 * it, 1, it), Head(2 + 2 * it, 0, it + 1), Head(3 + 2 * it, 1, it + 1)
        period(odd, even, False)
        period(even, odd2, False)
    period(static_head(heads - 1), None, True)


class Plan:

    def __init__(self, keys, packed):
        self.keys = keys
        self.tiles = -(-keys // P)
        wide = keys > N
        self.bufs = 6 if wide else 8
        self.lag = 4 if wide else 3
        self.evac = self.lag
        self.fold = self.lag + 1
        self.post, to_y, join, share = (20, 2, 0.6, 0.5) if wide else (7, 2, 0.3, 0.5) if packed else (7, 2, 1.0, 0.25)
        self.chunks = -(-keys // CHUNK)
        self.units = 2 * self.tiles
        max_jobs = [[("X", t, c) for t in range(NT)] for c in range(self.chunks)]
        if packed:
            seq = [j for c in max_jobs for j in c]
            self.copy_v = ("X", 0, self.chunks - 1)
        else:
            seq = [("Q", 0), ("K", 0)]
            for c, x in enumerate(max_jobs):
                seq += x[:2] + ([("Q", 1)] if c == 0 else [])
                seq += x[2:4] + ([("K", c + 1)] if c + 1 < self.chunks else [])
                seq += x[4:6] + [("V", c)] + x[6:]
        self.prep = seq + [("M", 0), ("M", 1)]
        self.filled_before = self.prep[0] if packed else ("M", 0)
        self.m_step = self.units - (2 if packed else 3)
        steps = [[] for _ in range(self.units)]
        for half in range(2):
            steps[self.m_step + half].append(("M", half))
        for half in range(2):
            at = (1 - half) * self.tiles + self.post
            steps[at].append(("D", half))
            steps[min(at + to_y, self.units - 1)].append(("Y", half))
        cost = {"X": 0.6, "K": 0.81, "V": 0.855, "Q": 0.9, "D": 0.9, "Y": 1.1, "M": 0.8}
        if packed:
            cost.update(X=0.48, D=0.49, Y=1.355, M=0.63)
        elif not wide:
            cost.update(K=1.125, D=1.134, M=0.9)
        before_shift = steps[:self.m_step]
        load = [sum(cost[j[0]] for j in st) for st in before_shift]
        for half_start in (0, self.tiles):
            if half_start + self.post <= self.m_step:
                load[half_start + self.post - 1] += join
        each = (sum(load) + sum(cost[j[0]] for j in seq)) / len(load)
        budget, todo = 0.0, list(seq)
        for at, st in enumerate(before_shift):
            budget += each - load[at]
            while todo and (budget >= cost[todo[0][0]] * share or at == len(load) - 1):
                if todo[0][0] == "V" and at <= self.lag:
                    break
                budget -= cost[todo[0][0]]
                st.append(todo.pop(0))
        self.steps = steps
        self.products = [[u - self.lag] for u in range(self.units)]
        for first in (0, self.tiles):
            late = first + self.lag
            self.products[late + 1] = self.products[late] + self.products[late + 1]
            self.products[late] = []
        order = [j for s in steps for j in s]
        self.local = {j: n for n, j in enumerate(order)}
        self.per_head = len(order)
        self.lead = len(self.prep)

    def job(self, head, job):
        return self.lead + head.h * self.per_head + self.local[job]

    def prep_job(self, head, job):
        if head.first:
            return self.prep.index(job)
        return self.job(head.back(1), job)

    def post_job(self, head, half, kind, heads):
        if half == 0:
            if self.ends(head, heads):
                return self.last_period_job(head, 0, kind)
            return self.job(head, (kind, 0))
        if self.ends(head, heads):
            return self.last_period_job(head, 1, kind) + 4
        after = Head(head.h + 1, 1 - head.par, None)
        return self.last_period_job(after, 1, kind) if self.ends(after, heads) else self.job(after, (kind, 1))

    @staticmethod
    def ends(head, heads):
        return isinstance(head.h, int) and head.h == heads - 1

    def last_period_job(self, head, half, kind):
        return self.lead + head.h * self.per_head + 2 * (1 - half) + (kind == "Y")

    def jobs_at(self, head, last, step):
        out = []
        for j in self.steps[step]:
            if j[0] in "DY":
                if j[1] == 1 and head.first:
                    out.append((self.job(head, j), ("none", j)))
                    continue
                if last:
                    out.append((self.last_period_job(head, j[1], j[0]), j))
                    continue
            elif last:
                continue
            out.append((self.job(head, j), j))
        return out

    def chunk_keys(self, c):
        return min(CHUNK, self.keys - c * CHUNK)

    def tile_keys(self, i):
        return min(P, self.keys - i * P)

    def unit(self, head, u):
        return head.h * self.units + u


def attention(nc, held, name, heads, keys, X, XT, ident, w, bias, ctx_dram=None, packed=None, scale=0.125):
    plan = Plan(keys, packed is not None)
    C = ctx_dram.shape[0] if ctx_dram is not None else P
    TILES, CHUNKS, UNITS = plan.tiles, plan.chunks, plan.units
    BUFS, LAG, POST_STEP = plan.bufs, plan.lag, plan.post
    EVAC_STEP = plan.evac
    KW = TILES * P
    with ExitStack() as ctx:
        def sb(n, shape, dt=F32):
            return ctx.enter_context(nc.sbuf_tensor(f"{name}_{n}", shape, dt))

        def sem(n):
            return held.enter_context(nc.semaphore(f"{name}_{n}"))

        KA = [sb(f"KA{i}", [P, KW], F32R) for i in range(2)]
        KB = [sb(f"KB{i}", [P, KW], F32R) for i in range(2)]
        QA = [sb(f"QA{i}", [P, N], F32R) for i in range(2)]
        QB = [sb(f"QB{i}", [P, N], F32R) for i in range(2)]
        V = [sb(f"V{i}", [P, TILES, VW], F32R) for i in range(2)]
        HI = [sb(f"HI{i}", [P, HALF], F32R) for i in range(BUFS)]
        LO = [sb(f"LO{i}", [P, HALF], F32R) for i in range(BUFS)]
        SUM = [sb(f"SUM{i}", [P, HALF]) for i in range(2)]
        ODD = sb("ODD", [P, HALF])
        OT = sb("OT", [P, HALF])
        OLO = sb("OLO", [P, HALF])
        RDEN = sb("RDEN", [P, HALF // P])
        MX = sb("MX", [P, NT, CHUNKS])
        NEGMAX = sb("NEGMAX", [P, NT])
        SHIFT = sb("SHIFT", [P, NT], F32R)
        WO = [sb(f"WO{i}", [P, D]) for i in range(2)]
        ones = sb("ones", [P, 8])
        BIAS = sb("BIAS", [P, D])
        if packed is None:
            WQ = sb("WQ", [P, P])
            WK = sb("WK", [P, P])
            WV = sb("WV", [P, E])
        if ctx_dram is not None:
            CTX = [sb(f"CTX{i}", [P, CHUNK]) for i in range(2)]
        if packed is not None:
            VH, VL = packed["vh"], packed["vl"]

        def bank(n):
            return ctx.enter_context(nc.psum_tensor(f"{name}_{n}", [P, 512], F32))

        S = [bank(f"S{i}") for i in range(SLOTS)]
        OA, OB = bank("OA"), bank("OB")
        SIDE = [bank(f"SIDE{i}") for i in range(2)]

        filled = [sem(f"filled{i}") for i in range(2)]
        ones_set = sem("ones_set")
        bias_in = sem("bias_in")
        bias_added = sem("bias_added")
        w_in = sem("w_in")
        wo_in = [sem(f"wo_in{i}") for i in range(2)]
        ctx_in = [sem(f"ctx_in{i}") for i in range(2)]
        kb_in = [sem(f"kb_in{i}") for i in range(2)]
        side_done = sem("side_done")
        side_act = sem("side_act")
        side_free = sem("side_free")
        s_done = sem("s_done")
        hi_done = sem("hi_done")
        p_done = sem("p_done")
        lo_done = sem("lo_done")
        pv_done = sem("pv_done")
        sum_done = sem("sum_done")
        folded = sem("folded")
        evac = sem("evac")
        joined = sem("joined")
        max_step = sem("max_step")

        ACT_PER_HEAD = 2 + 2 * CHUNKS
        act_order = [j for j in plan.prep if j[0] in "QKV"]

        def act_count(head, job):
            return head.h * ACT_PER_HEAD + act_order.index(job) + 1

        SUMS = TILES - 2

        def sums_before(head, half, i):
            return (2 * head.h + half) * SUMS + (i + 1 if i < 2 else i - 1)

        def ctx_slot(head, c):
            return (head.par * CHUNKS + c) % 2

        def ctx_count(head, c):
            return 16 * (CHUNKS * head.hp + (head.par * CHUNKS + c) // 2 + 1)

        KB_DMAS = CHUNKS if packed is None else 6

        def unit_slot(head, u):
            return (head.par * UNITS + u) % SLOTS

        def unit_buf(head, u):
            return (head.par * UNITS + u) % BUFS

        assert 2 * UNITS % SLOTS == 0 and 2 * UNITS % BUFS == 0

        def v_parts(c):
            t0 = c * CHUNK // P
            t1 = min(t0 + CHUNK // P, TILES)
            full = keys // P
            out = [(P, t0, min(t1, full))] if min(t1, full) > t0 else []
            if t1 > full:
                out.append((keys - full * P, full, t1))
            return out

        def v_offset(c, t):
            return t - c * CHUNK // P

        def side_bank(n, job, first):
            if first:
                return (SIDE + S)[n % (2 + SLOTS)]
            return SIDE[n % 2 if isinstance(n, int) else bank_of[job[1] if job[0] == 'none' else job]]

        assert plan.per_head % 2 == 0
        bank_of = {j: (plan.lead + k) % 2 for j, k in plan.local.items()}
        assert plan.lead % 2 == 0

        def fill(eng, i):
            fills = [(KB[i][LO0:P, :], 1.0), (QB[i][LO0:P, :], 0.0), (V[i][:, :, 2 * E:VW], 1.0)]
            if packed is not None:
                fills += [(KA[i][:], 0.0), (KB[i][0:LO0, :], 0.0), (QA[i][:], 0.0), (QB[i][0:LO0, :], 0.0),
                          (V[i][:, :, 0:2 * E], 0.0), (V[i][:, :, SUM_ROW:SUM_ROW + 1], 1.0)]
            elif KW > keys:
                fills += [(KA[i][:, keys:KW], 0.0), (KB[i][0:LO0, keys:KW], 0.0)]
            for n, (rows, value) in enumerate(fills):
                if n:
                    eng.wait_ge(filled[i], n)
                eng.memset(rows.bitcast(F32), value).then_inc(filled[i], 1)

        low_sums = slice(0, 1) if packed is None else slice(SUM_ROW, SUM_ROW + 1)
        FILLS = 3 + (6 if packed is not None else 2 if KW > keys else 0)

        with nc.Block() as block:

            @block.sync
            def _(sp):
                sp.dma_start(BIAS[:], bias.partition_broadcast(P)).then_inc(bias_in, 16)

                def load_wo(head, free):
                    if not head.early:
                        sp.wait_ge(side_done, free)
                    sp.dma_start(WO[head.par][:], w[3][head.h, :, :]).then_inc(wo_in[head.par], 16)

                def prepare(head):
                    par = head.par
                    if packed is None:
                        if not head.first:
                            sp.wait_ge(side_done, plan.prep_job(head.back(1), ("V", CHUNKS - 1)) + 1)
                        sp.dma_start(WQ[:], w[0][head.h, :, :]).then_inc(w_in, 16)
                        sp.dma_start(WK[0:C, :], w[1][head.h, :, :]).then_inc(w_in, 16)
                        sp.dma_start(WV[0:C, :], w[2][head.h, :, :]).then_inc(w_in, 16)

                        def load_ctx(c):
                            if c >= 2:
                                sp.wait_ge(side_done, plan.prep_job(head, ("V", c - 2)) + 1)
                            sp.dma_start(CTX[ctx_slot(head, c)][0:C, 0:plan.chunk_keys(c)],
                                         ctx_dram[:, c * CHUNK:c * CHUNK + plan.chunk_keys(c)])\
                              .then_inc(ctx_in[ctx_slot(head, c)], 16)

                        if ctx_dram is not None:
                            load_ctx(0)
                            load_ctx(1)
                        for c in range(CHUNKS):
                            sp.wait_ge(side_act, act_count(head, ("K", c)))
                            k = slice(c * CHUNK, c * CHUNK + plan.chunk_keys(c))
                            sp.dma_start(KB[par][0:E, k].bitcast(F32), KA[par][0:E, k].bitcast(F32)).then_inc(kb_in[par], 16)
                            if ctx_dram is not None and c + 2 < CHUNKS:
                                load_ctx(c + 2)
                    else:
                        if head.early:
                            sp.wait_ge(filled[par], FILLS)
                        if not head.early:
                            sp.wait_ge(s_done, plan.unit(head.back(1), 0))
                        for dst, src in ((KA[par][0:8, :], "kh"), (KA[par][LO0:LO0 + 8, :], "kl"),
                                         (KB[par][0:8, :], "kh"), (QA[par][0:8, :], "qh"),
                                         (QA[par][LO0:LO0 + 8, :], "qh"), (QB[par][0:8, :], "ql")):
                            sp.dma_start(dst.bitcast(F32), packed[src][head.h, :, :]).then_inc(kb_in[par], 16)

                prepare(static_head(0))
                load_wo(static_head(0), None)

                def period(head, nxt, last):
                    if last:
                        return
                    if packed is not None and head.first:
                        sp.wait_ge(filled[1], FILLS)
                    prepare(nxt)
                    load_wo(nxt, plan.job(head, ("Y", 1)) + 1 if not head.first else None)

                over_heads(sp, heads, period)

            @block.gpsimd
            def _(pool):
                if packed is None:
                    fill(pool, 0)
                    pool.wait_ge(filled[0], FILLS)
                fill(pool, 1)
                pool.wait_ge(filled[1], FILLS)

                def merge(head, half):
                    pool.wait_ge(sum_done, (2 * head.h + half + 1) * SUMS)
                    pool.tensor_tensor(SUM[half][:], SUM[half][:], ODD[:], ALU.add).then_inc(folded, 1)

                def fold(head, half):
                    pool.wait_ge(folded, 2 * (2 * head.h + half) + 1)
                    pool.wait_ge(evac, 2 * head.h + half + 1)
                    pool.tensor_tensor(SUM[half][0:1, :], SUM[half][0:1, :], OLO[low_sums, :], ALU.add).then_inc(folded, 1)

                def period(head, nxt, last):
                    for half in range(2):
                        before = (head, 0) if half else (head.back(1), 1)
                        if half or not head.first:
                            merge(*before)
                        for i in range(2, TILES):
                            u = half * TILES + i
                            kp = plan.tile_keys(i)
                            if i == plan.fold and (half or not head.first):
                                fold(*before)
                            acc = ODD if i % 2 else SUM[half]
                            hi = HI[unit_buf(head, u)][0:kp, :].bitcast(F32)
                            pool.wait_ge(hi_done, plan.unit(head, u) + 1)
                            if i < 4:
                                if not head.first:
                                    pool.wait_ge(side_done, plan.post_job(head.back(1), half, "D", heads) + 1)
                                if i == 3 and (half or not head.first):
                                    pool.wait_ge(folded, 2 * (2 * before[0].h + before[1]) + 1)
                                pool.tensor_tensor(acc[0:kp, :], HI[unit_buf(head, u - 2)][0:kp, :].bitcast(F32), hi,
                                                   ALU.add).then_inc(sum_done, 1)
                            else:
                                pool.wait_ge(sum_done, sums_before(head, half, i - 2))
                                pool.tensor_tensor(acc[0:kp, :], acc[0:kp, :], hi, ALU.add).then_inc(sum_done, 1)

                if packed is None:
                    over_heads(pool, heads, period)
                    merge(static_head(heads - 1), 1)
                    fold(static_head(heads - 1), 1)

            @block.scalar
            def _(act):
                def side(head, n, job, preparing=False):
                    if job[0] not in ("Q", "K", "V"):
                        return
                    act.wait_ge(side_done, n + 1)
                    ps = side_bank(n, job, preparing)
                    par = head.par
                    if job[0] == "Q":
                        act.activation(QA[par][:, job[1] * HALF:(job[1] + 1) * HALF], ps[:], ACT.Copy,
                                       scale=scale).then_inc(side_act, 1)
                    elif job[0] == "K":
                        m = plan.chunk_keys(job[1])
                        act.activation(KA[par][:, job[1] * CHUNK:job[1] * CHUNK + m], ps[:, 0:m], ACT.Copy)\
                           .then_inc(side_act, 1)
                    else:
                        if not head.early:
                            act.wait_ge(pv_done, plan.unit(head.back(1), 0))
                        last = None
                        for rows, t0, t1 in v_parts(job[1]):
                            o = v_offset(job[1], t0)
                            src = ps[0:rows, o * E:(o + t1 - t0) * E]
                            last = act.activation(V[par][0:rows, t0:t1, E:2 * E],
                                                  src.rearrange("p (t e) -> p t e", e=E), ACT.Copy)
                        last.then_inc(side_act, 1)

                def take_output(head, half):
                    act.wait_ge(pv_done, plan.unit(head, (half + 1) * TILES))
                    if not (head.first and half == 0):
                        before = (head, 0) if half else (head.back(1), 1)
                        act.wait_ge(side_done, plan.post_job(*before, "Y", heads) + 1)
                    act.activation(OT[:], OA[:], ACT.Copy)
                    act.activation(OLO[LO0:P, :], OB[0:E, :], ACT.Copy)
                    act.activation(OLO[low_sums, :], OB[LO0:LO0 + 1, :], ACT.Copy).then_inc(evac, 1)

                h0 = static_head(0)
                for n, job in enumerate(plan.prep):
                    side(h0, n, job, True)

                def period(head, nxt, last):
                    for u in range(UNITS):
                        half, i = divmod(u, TILES)
                        kp = plan.tile_keys(i)
                        g = plan.unit(head, u)
                        slot = unit_slot(head, u)
                        if u == EVAC_STEP and not head.first:
                            take_output(head.back(1), 1)
                        if u == TILES + EVAC_STEP:
                            take_output(head, 0)
                        act.wait_ge(s_done, g + 1)
                        buf = unit_buf(head, u)
                        if not (head.first and u < BUFS):
                            act.wait_ge(pv_done, g - BUFS + 1)
                            b = u - BUFS
                            owner, b_half, b_tile = (head.back(1), 1, b + TILES) if b < 0 else (head, *divmod(b, TILES))
                            if packed is None:
                                act.wait_ge(sum_done, sums_before(owner, b_half, b_tile))
                        act.activation(HI[buf][0:kp, :], S[slot][0:kp, :], ACT.Exp).then_inc(hi_done, 1)
                        for n, job in plan.jobs_at(head, last, u):
                            side(nxt, n, job)
                        act.activation(S[slot][0:kp, :], S[slot][0:kp, :], ACT.Exp).then_inc(p_done, 1)

                over_heads(act, heads, period)
                take_output(static_head(heads - 1), 1)

            @block.vector
            def _(dve):
                dve.memset(ones[:], 1.0).then_inc(ones_set, 1)
                if packed is not None:
                    fill(dve, 0)
                dve.wait_ge(bias_in, 16)
                dve.tensor_tensor(X[:], X[:], BIAS[:].unsqueeze(1).broadcast_to([P, NT, D]), ALU.add)\
                   .then_inc(bias_added, 1)

                def side(head, n, job, preparing=False):
                    if job[0] == "none":
                        dve.wait_ge(side_done, n + 1)
                        dve.wait_ge(side_free, n)
                        dve.engine_nop().then_inc(side_free, 1)
                        return
                    ps = side_bank(n, job, preparing)
                    kind = job[0]
                    par = head.par if head is not None else None
                    if kind in "QKV":
                        dve.wait_ge(side_done, n + 1)
                        dve.wait_ge(side_act, act_count(head, job))
                        if kind == "Q":
                            q = slice(job[1] * HALF, (job[1] + 1) * HALF)
                            dve.scalar_tensor_tensor(QB[par][0:E, q], ps[0:E, :], scale, QA[par][0:E, q].bitcast(F32),
                                                     ALU.mult, ALU.subtract).then_inc(side_free, 1)
                        elif kind == "K":
                            m = plan.chunk_keys(job[1])
                            k = slice(job[1] * CHUNK, job[1] * CHUNK + m)
                            dve.tensor_tensor(KA[par][LO0:P, k], ps[LO0:P, 0:m], KA[par][LO0:P, k].bitcast(F32),
                                              ALU.subtract).then_inc(side_free, 1)
                        else:
                            last = None
                            for rows, t0, t1 in v_parts(job[1]):
                                o = v_offset(job[1], t0)
                                last = dve.tensor_tensor(
                                    V[par][0:rows, t0:t1, 0:E],
                                    ps[0:rows, o * E:(o + t1 - t0) * E].rearrange("p (t e) -> p t e", e=E),
                                    V[par][0:rows, t0:t1, E:2 * E].bitcast(F32), ALU.subtract)
                            last.then_inc(side_free, 1)
                    elif kind == "X":
                        if packed is not None and job == plan.copy_v:
                            if not head.early:
                                dve.wait_ge(pv_done, plan.unit(head.back(1), 0))
                            dve.tensor_copy(V[par][:, :, 0:8], VL[:, :, bass.ds(head.h * 8, 8)].bitcast(F32))
                            dve.tensor_copy(V[par][:, :, E:E + 8], VH[:, :, bass.ds(head.h * 8, 8)].bitcast(F32))
                        dve.wait_ge(side_done, n + 1)
                        dve.tensor_reduce(MX[:, job[1], job[2]:job[2] + 1], ps[:, 0:plan.chunk_keys(job[2])],
                                          AX.X, ALU.max).then_inc(side_free, 1)
                    elif kind == "M":
                        dve.wait_ge(side_done, n + 1)
                        q = slice(job[1] * HALF, (job[1] + 1) * HALF)
                        dve.tensor_copy(QB[par][LO0:LO0 + 1, q], ps[0:1, :]).then_inc(side_free, 1)
                    elif kind == "D":
                        dve.wait_ge(side_done, n + 1)
                        dve.reciprocal(RDEN[:], ps[:, 0:HALF // P]).then_inc(side_free, 1)
                    elif kind == "Y":
                        dve.wait_ge(side_done, n + 1)
                        dve.wait_ge(side_free, n)
                        dve.wait_ge(bias_added, 1)
                        last = None
                        for t in range(HALF // P):
                            xt = X[:, job[1] * (HALF // P) + t, :]
                            last = dve.scalar_tensor_tensor(xt, ps[:, t * D:(t + 1) * D], RDEN[:, t:t + 1], xt,
                                                            ALU.mult, ALU.add)
                        last.then_inc(side_free, 1)

                def shift(head):
                    dve.wait_ge(side_free, plan.prep_job(head, ("M", 0)))
                    dve.tensor_reduce(NEGMAX[:], MX[:], AX.X, ALU.max, negate=True).then_inc(max_step, 1)
                    dve.wait_ge(max_step, 2 * head.h + 1)
                    dve.tensor_copy(SHIFT[:], NEGMAX[:]).then_inc(max_step, 1)

                def join(head, half):
                    dve.wait_ge(evac, 2 * head.h + half + 1)
                    dve.tensor_tensor(OT[LO0:P, :], OLO[LO0:P, :], OT[LO0:P, :], ALU.add).then_inc(joined, 1)

                def low_part(head, u):
                    kp = plan.tile_keys(u % TILES)
                    slot = unit_slot(head, u)
                    g = plan.unit(head, u)
                    dve.wait_ge(p_done, g + 1)
                    buf = unit_buf(head, u)
                    if not (head.first and u < BUFS):
                        dve.wait_ge(pv_done, g - BUFS + 1)
                    dve.tensor_tensor(LO[buf][0:kp, :], S[slot][0:kp, :], HI[buf][0:kp, :].bitcast(F32),
                                      ALU.subtract).then_inc(lo_done, 1)

                h0 = static_head(0)
                for n, job in enumerate(plan.prep):
                    if job == plan.filled_before:
                        dve.wait_ge(filled[0], FILLS)
                    if job == ("M", 0):
                        shift(h0)
                    side(h0, n, job, True)
                dve.wait_ge(filled[1], FILLS)

                def period(head, nxt, last):
                    for u in range(UNITS):
                        if u == POST_STEP - 1 and not head.first:
                            join(head.back(1), 1)
                        if u == TILES + POST_STEP - 1:
                            join(head, 0)
                        jobs = plan.jobs_at(head, last, u)
                        cut = next((k for k, (_, job) in enumerate(jobs) if job[0] in ("Q", "K", "V")), len(jobs))
                        for n, job in jobs[:cut]:
                            side(nxt, n, job)
                        if u >= LOW_LAG:
                            low_part(head, u - LOW_LAG)
                        elif not head.first:
                            low_part(head.back(1), UNITS + u - LOW_LAG)
                        for n, job in jobs[cut:]:
                            side(nxt, n, job)
                        if u == plan.m_step - 1 and not last:
                            shift(nxt)

                over_heads(dve, heads, period)
                end = static_head(heads - 1)
                for u in range(UNITS - LOW_LAG, UNITS):
                    low_part(end, u)
                join(end, 1)
                for kind in "DY":
                    side(None, plan.post_job(end, 1, kind, heads), (kind, 1))

            @block.tensor
            def _(pe):
                def side(head, done, n, job, preparing=False):
                    ps = side_bank(n, job, preparing)
                    kind = job[0]
                    par = head.par if head is not None else None
                    if preparing:
                        if n >= 2 + SLOTS:
                            pe.wait_ge(side_free, n - SLOTS - 1)
                    else:
                        pe.wait_ge(side_free, n - 1)
                    if kind == "none":
                        last = pe.matmul(ps[0:1, 0:1], ident[:, 0:1], ident[:, 0:1], start=True, stop=True)
                    elif kind == "Q":
                        pe.wait_ge(w_in, 48 * (head.h + 1))
                        last = pe.matmul(ps[:], WQ[:], XT[:, job[1] * HALF:(job[1] + 1) * HALF], start=True, stop=True)
                    elif kind in "KV":
                        c = job[1]
                        m = plan.chunk_keys(c)
                        if ctx_dram is not None:
                            slot = ctx_slot(head, c)
                            pe.wait_ge(ctx_in[slot], ctx_count(head, c))
                            src = CTX[slot][0:C, 0:m]
                        else:
                            src = XT[:, c * CHUNK:c * CHUNK + m]
                        if kind == "K":
                            last = pe.matmul(ps[:, 0:m], WK[0:C, :], src, start=True, stop=True)
                        else:
                            for j in range(-(-m // P)):
                                rows = min(P, m - j * P)
                                last = pe.matmul(ps[0:rows, j * E:(j + 1) * E], src[:, j * P:j * P + rows],
                                                 WV[0:C, :], start=True, stop=True)
                    elif kind == "X":
                        t, c = job[1:]
                        m = plan.chunk_keys(c)
                        if packed is None:
                            latest = ("Q", 1) if c == 0 and t >= NT // 2 else ("K", c)
                            pe.wait_ge(side_free, plan.prep_job(head, latest) + 1)
                        else:
                            pe.wait_ge(kb_in[par], 16 * KB_DMAS * (head.hp + 1))
                        last = pe.matmul(ps[:, 0:m], QA[par][:, t * P:(t + 1) * P],
                                         KA[par][:, c * CHUNK:c * CHUNK + m], start=True, stop=True)
                    elif kind == "M":
                        pe.wait_ge(max_step, 2 * head.h + 2)
                        for j in range(HALF // P):
                            t = job[1] * (HALF // P) + j
                            last = pe.matmul(ps[0:1, j * P:(j + 1) * P], SHIFT[:, t:t + 1].bitcast(F32), ident[:],
                                             start=True, stop=True)
                    elif kind == "D":
                        if packed is None:
                            pe.wait_ge(folded, 2 * (2 * done.h + job[1] + 1))
                        else:
                            pe.wait_ge(evac, 2 * done.h + job[1] + 1)
                        for t in range(HALF // P):
                            q, den = slice(t * P, (t + 1) * P), ps[:, t:t + 1]
                            if packed is None:
                                last = pe.matmul(den, SUM[job[1]][:, q], ones[:, 0:1], start=True, stop=True)
                            else:
                                pe.matmul(den, OT[low_sums, q], ones[low_sums, 0:1], start=True, stop=False)
                                last = pe.matmul(den, OLO[low_sums, q], ones[low_sums, 0:1], start=False, stop=True)
                    elif kind == "Y":
                        pe.wait_ge(joined, 2 * done.h + job[1] + 1)
                        pe.wait_ge(wo_in[done.par], 16 * (done.hp + 1))
                        for t in range(HALF // P):
                            last = pe.matmul(ps[:, t * D:(t + 1) * D], OT[:, t * P:(t + 1) * P], WO[done.par][:],
                                             start=True, stop=True)
                    last.then_inc(side_done, 1)

                def scores(head, u):
                    half, i = divmod(u, TILES)
                    slot = unit_slot(head, u)
                    g = plan.unit(head, u)
                    if u == 0:
                        prep_done = plan.prep_job(head, ("M", 1)) + 1
                        pe.wait_ge(side_free, prep_done)
                        pe.wait_ge(kb_in[head.par], 16 * KB_DMAS * (head.hp + 1))
                    if not (head.first and u < SLOTS):
                        pe.wait_ge(lo_done, g - SLOTS + 1)
                    k = slice(i * P, (i + 1) * P)
                    q = slice(half * HALF, (half + 1) * HALF)
                    pe.matmul(S[slot][:], KA[head.par][:, k], QA[head.par][:, q], start=True, stop=False)
                    pe.matmul(S[slot][:], KB[head.par][:, k], QB[head.par][:, q], start=False, stop=True)\
                      .then_inc(s_done, 1)

                def product(head, u):
                    half, i = divmod(u, TILES)
                    kp = plan.tile_keys(i)
                    buf = unit_buf(head, u)
                    g = plan.unit(head, u)
                    ends = dict(start=i == 0, stop=i == TILES - 1)
                    if i == 0 and not (head.first and half == 0):
                        pe.wait_ge(evac, 2 * head.h + half)
                    pe.wait_ge(lo_done, g + 1)
                    pe.matmul(OA[:], V[head.par][0:kp, i, 0:2 * E], HI[buf][0:kp, :], **ends)
                    pe.matmul(OB[0:E + 1, :], V[head.par][0:kp, i, E:VW], LO[buf][0:kp, :], **ends)\
                      .then_inc(pv_done, 1)

                h0 = static_head(0)
                for n, job in enumerate(plan.prep):
                    side(h0, None, n, job, True)
                pe.wait_ge(filled[0], FILLS)
                pe.wait_ge(filled[1], FILLS)
                pe.wait_ge(ones_set, 1)

                def period(head, nxt, last):
                    for u in range(UNITS):
                        scores(head, u)
                        for n, job in plan.jobs_at(head, last, u):
                            side(nxt, head.back(1) if job in (("D", 1), ("Y", 1)) else head, n, job)
                        for v in plan.products[u]:
                            if v >= 0:
                                product(head, v)
                            elif not head.first:
                                product(head.back(1), UNITS + v)

                over_heads(pe, heads, period)
                end = static_head(heads - 1)
                for u in range(UNITS - LAG, UNITS):
                    product(end, u)
                for kind in "DY":
                    side(None, end, plan.post_job(end, 1, kind, heads), (kind, 1))


class NormSemaphores:

    def __init__(self, nc, held):
        self.loaded, self.stats, self.var_in, self.rstd, self.normed, self.turned, self.copied = [
            held.enter_context(nc.semaphore(f"norm_{n}"))
            for n in ("loaded", "stats", "var_in", "rstd", "normed", "turned", "copied")]
        self.norms = 0


def layer_norm(nc, sems, name, eps, src, XH, XT, ident, load=None):
    with ExitStack() as ctx:
        def sb(n, shape, dt=F32):
            return ctx.enter_context(nc.sbuf_tensor(f"{name}_{n}", shape, dt))

        STATS = sb("STATS", [P, NT, 6])
        MV = sb("MV", [P, NT, 2])
        VE = sb("VE", [P, NT])
        POWER = sb("POWER", [P, NT])
        RSTD = sb("RSTD", [P, NT])
        T = [ctx.enter_context(nc.psum_tensor(f"{name}_T{i}", [P, 512], F32)) for i in range(2)]
        k = sems.norms
        sems.norms += 1

        with nc.Block() as block:

            if load is not None:
                @block.sync
                def _(sp):
                    for dst, dram in load:
                        sp.dma_start(dst, dram).then_inc(sems.loaded, 16)

            @block.vector
            def _(dve):
                if load is not None:
                    dve.wait_ge(sems.loaded, 16 * len(load))
                for t in range(NT):
                    dve.bn_stats(STATS[:, t, :], src[:, t, :]).then_inc(sems.stats, 1)
                for t in range(NT):
                    dve.wait_ge(sems.stats, 2 * NT * k + t + 1)
                    dve.bn_aggr(MV[:, t, :], STATS[:, t, :]).then_inc(sems.stats, 1)
                dve.wait_ge(sems.stats, 2 * NT * (k + 1))
                dve.memset(POWER[:], -0.5)
                dve.tensor_scalar(VE[:], MV[:, :, 1], eps, None, ALU.add).then_inc(sems.var_in, 1)
                dve.wait_ge(sems.rstd, k + 1)
                for t in range(NT):
                    dve.tensor_scalar(XH[:, t, :], src[:, t, :], MV[:, t, 0:1], RSTD[:, t:t + 1],
                                      ALU.subtract, ALU.mult).then_inc(sems.normed, 1)
                dve.wait_ge(sems.turned, 2 * k + 1)
                dve.tensor_copy(XT[:, 0:512], T[0][:]).then_inc(sems.copied, 1)

            @block.gpsimd
            def _(pool):
                pool.wait_ge(sems.var_in, k + 1)
                pool.tensor_tensor(RSTD[:], VE[:], POWER[:], ALU.pow).then_inc(sems.rstd, 1)

            @block.tensor
            def _(pe):
                for t in range(NT):
                    pe.wait_ge(sems.normed, NT * k + t + 1)
                    last = pe.transpose(T[t // 4][:, t % 4 * P:(t % 4 + 1) * P], XH[:, t, :], ident[:])
                    if t % 4 == 3:
                        last.then_inc(sems.turned, 1)

            @block.scalar
            def _(act):
                act.wait_ge(sems.turned, 2 * k + 2)
                act.activation(XT[:, 512:1024], T[1][:], ACT.Copy).then_inc(sems.copied, 1)


def rotary(nc, held, name, XT, w_dram, tables, scratch, VH, VL, scale):
    with ExitStack() as ctx:
        def sb(n, shape, dt=F32):
            return ctx.enter_context(nc.sbuf_tensor(f"{name}_{n}", shape, dt))

        def sem(n):
            return held.enter_context(nc.semaphore(f"{name}_{n}"))

        W = [sb(f"W{i}", [P, P]) for i in range(4)]
        COS, SIN = sb("COS", [P, N]), sb("SIN", [P, N])
        COSV, SINV = sb("COSV", [P, NT, P]), sb("SINV", [P, NT, P])
        A = [sb(f"A{i}", [P, N]) for i in range(3)]
        B = [sb(f"B{i}", [P, N]) for i in range(3)]
        PARTS = {n: sb(n, [P, N], F32R) for n in ("qh", "ql", "kh", "kl")}
        BANK = [ctx.enter_context(nc.psum_tensor(f"{name}_BANK{i}", [P, 512], F32)) for i in range(8)]
        w_in, projected, step, out = sem("w_in"), sem("projected"), sem("step"), sem("out")

        with nc.Block() as block:

            @block.sync
            def _(sp):
                for i in range(4):
                    sp.dma_start(W[i][:], w_dram[i]).then_inc(w_in, 16)
                sp.dma_start(COS[:], tables[0]).then_inc(w_in, 16)
                sp.dma_start(SIN[:], tables[1]).then_inc(w_in, 16)
                sp.dma_start(COSV[:], tables[2].rearrange("(t p) d -> p t d", p=P)).then_inc(w_in, 16)
                sp.dma_start(SINV[:], tables[3].rearrange("(t p) d -> p t d", p=P)).then_inc(w_in, 16)
                sp.wait_ge(step, 20)
                for n in ("qh", "ql", "kh", "kl"):
                    sp.dma_start(scratch[n].rearrange("h d n -> (h d) n"), PARTS[n][:].bitcast(F32)).then_inc(out, 16)
                sp.wait_ge(out, 64)

            @block.tensor
            def _(pe):
                pe.wait_ge(w_in, 128)
                for i in range(4):
                    for half in range(2):
                        pe.matmul(BANK[2 * i + half][:], W[i][:], XT[:, half * 512:(half + 1) * 512],
                                  start=True, stop=True).then_inc(projected, 1)
                pe.wait_ge(step, 4)
                for t in range(NT):
                    for i in range(2):
                        pe.matmul(BANK[2 * i + t // 4][:, t % 4 * P:(t % 4 + 1) * P], XT[:, t * P:(t + 1) * P],
                                  W[2 + i][:], start=True, stop=True).then_inc(projected, 1)

            @block.vector
            def _(dve):
                count = 0

                def turn(b0, a, b, cos, sin):
                    for half in range(2):
                        h = slice(half * 512, (half + 1) * 512)
                        dve.tensor_tensor(a[:, h], BANK[b0 + half][:], cos[:, h], ALU.mult).then_inc(step, 1)
                        dve.tensor_tensor(b[:, h], BANK[b0 + 2 + half][:], sin[:, h], ALU.mult).then_inc(step, 1)

                flat = [t[:].rearrange("p t d -> p (t d)") for t in (COSV, SINV)]
                dve.wait_ge(w_in, 128)
                dve.wait_ge(projected, 8)
                turn(0, A[0], B[0], COS[:], SIN[:])
                turn(4, A[1], B[1], COS[:], SIN[:])
                dve.wait_ge(projected, 8 + 2 * NT)
                turn(0, A[2], B[2], flat[0], flat[1])
                dve.wait_ge(step, 12)
                for i in range(3):
                    dve.tensor_tensor(A[i][:], A[i][:], B[i][:], ALU.add).then_inc(step, 1)
                dve.wait_ge(step, 15)
                dve.tensor_scalar(B[0][:], A[0][:], scale, None, ALU.mult).then_inc(step, 1)
                dve.wait_ge(step, 16)
                hi = (PARTS["qh"][:], PARTS["kh"][:], VH[:].rearrange("p t d -> p (t d)"))
                lo = (PARTS["ql"][:], PARTS["kl"][:], VL[:].rearrange("p t d -> p (t d)"))
                x = (B[0], A[1], A[2])
                for i in range(3):
                    last = dve.tensor_copy(hi[i], x[i][:])
                last.then_inc(step, 1)
                dve.wait_ge(step, 17)
                for i in range(3):
                    dve.tensor_tensor(lo[i], x[i][:], hi[i].bitcast(F32), ALU.subtract).then_inc(step, 1)


def experts(nc, held, name, count, gated, X, XH, XT, ident, dram, func, normed):
    XT_in = normed if normed is not None else XT
    F = 512
    KF = F // P
    with ExitStack() as ctx:
        def sb(n, shape, dt=F32):
            return ctx.enter_context(nc.sbuf_tensor(f"{name}_{n}", shape, dt))

        def sem(n):
            return held.enter_context(nc.semaphore(f"{name}_{n}"))

        G = gated
        GW = sb("GW", [P, G])
        GB = sb("GB", [P, G])
        B2 = sb("B2", [16, D])
        W1 = [sb(f"W1{i}", [P, F]) for i in range(2)]
        W2 = [sb(f"W2{i}", [P, KF, D]) for i in range(2)]
        B1 = [sb(f"B1{i}", [P, KF]) for i in range(2)]
        AFF = [sb(f"AFF{i}", [P, 2]) for i in range(2)]
        XE = [sb(f"XE{i}", [P, N]) for i in range(2)] if normed is not None else [XT, XT]
        H = [sb(f"H{i}", [P, KF, N]) for i in range(2)]
        WE = [sb(f"WE{i}", [P, NT]) for i in range(2)]
        ACC = sb("ACC", [P, NT, D])
        WT = sb("WT", [16, N])
        R = {n: sb(n, [P, NT, G]) for n in ("score", "prob", "eq", "one1", "one2", "rest", "tmp")}
        REV = sb("REV", [P, NT, G])
        WALL = sb("WALL", [P, NT, count])
        C = {n: sb(n, [P, NT]) for n in ("m", "neg", "den", "rden", "v1", "v2", "pos", "sum", "e", "w1", "w2")}
        UP = [ctx.enter_context(nc.psum_tensor(f"{name}_UP{i}", [P, 512], F32)) for i in range(4)]
        DN = [ctx.enter_context(nc.psum_tensor(f"{name}_DN{i}", [P, 512], F32)) for i in range(4)]
        const_in, logits, r, exp_done, turned, wt, b2_done, acc0 = [
            sem(n) for n in ("const_in", "logits", "r", "exp_done", "turned", "wt", "b2_done", "acc0")]
        w1_in = [sem(f"w1_in{i}") for i in range(2)]
        w2_in = [sem(f"w2_in{i}") for i in range(2)]
        up_done, h_done, dn_done, acc_done, xe_done, x_done = [
            sem(n) for n in ("up_done", "h_done", "dn_done", "acc_done", "xe_done", "x_done")]
        PER_W = 16 * (3 if normed is not None else 2)

        def loop(eng, body):
            with eng.Fori(0, (count - 2) // 2) as it:
                body(2 * it, 0, it)
                body(2 * it + 1, 1, it)
            for e in range((count - 2) // 2 * 2, count - 2):
                body(e, e % 2, e // 2)

        last_two = [(e, e % 2, e // 2) for e in (count - 2, count - 1)]

        with nc.Block() as block:

            @block.sync
            def _(sp):
                sp.dma_start(GW[:], dram["gate"]).then_inc(const_in, 16)
                if dram["gate_b"] is not None:
                    sp.dma_start(GB[:], dram["gate_b"].partition_broadcast(P)).then_inc(const_in, 16)
                sp.dma_start(B2[0:count, :], dram["b2"]).then_inc(const_in, 16)

                def load_up(e, par):
                    sp.dma_start(W1[par][:], dram["w1"][e, :, :]).then_inc(w1_in[par], 16)
                    sp.dma_start(B1[par][:], dram["b1"][e, :, :]).then_inc(w1_in[par], 16)
                    if normed is not None:
                        sp.dma_start(AFF[par][:], dram["affine"][e, :, :]).then_inc(w1_in[par], 16)

                def load_down(e, par):
                    sp.dma_start(W2[par][:], dram["w2"][e, :, :, :]).then_inc(w2_in[par], 16)

                for e in range(2):
                    load_up(e, e)
                for e in range(2):
                    load_down(e, e)

                def body(e, par, ep):
                    sp.wait_ge(h_done, 8 * e + 8)
                    load_up(e + 2, par)
                    sp.wait_ge(dn_done, 2 * e + 2)
                    load_down(e + 2, par)

                loop(sp, body)

            @block.tensor
            def _(pe):
                pe.wait_ge(const_in, 16 * (2 + (dram["gate_b"] is not None)))
                for t in range(NT):
                    last = pe.matmul(DN[3][:, t * G:(t + 1) * G], XT[:, t * P:(t + 1) * P], GW[:], start=True, stop=True)
                last.then_inc(logits, 1)
                def up(e, par, ep):
                    pe.wait_ge(w1_in[par], PER_W * (ep + 1))
                    if normed is not None:
                        pe.wait_ge(xe_done, e + 1)
                    for k in range(KF):
                        for half in range(2):
                            j = 2 * k + half
                            if not (isinstance(e, int) and e == 0 and j < 4):
                                pe.wait_ge(h_done, 8 * e + j - 3)
                            pe.matmul(UP[j % 4][:], W1[par][:, k * P:(k + 1) * P],
                                      XE[par][:, half * 512:(half + 1) * 512], start=True, stop=True)\
                              .then_inc(up_done, 1)

                def down(e, par, ep):
                    pe.wait_ge(h_done, 8 * e + 8)
                    pe.wait_ge(w2_in[par], 16 * (ep + 1))
                    for g in range(2):
                        if not isinstance(e, int) or e >= 2:
                            pe.wait_ge(acc_done, 2 * e + g - 3 + 4)
                        for j in range(4):
                            t = 4 * g + j
                            for k in range(KF):
                                last = pe.matmul(DN[2 * par + g][:, j * D:(j + 1) * D], H[par][:, k, t * P:(t + 1) * P],
                                                 W2[par][:, k, :], start=k == 0, stop=k == KF - 1)
                        last.then_inc(dn_done, 1)

                up(0, 0, 0)
                up(1, 1, 0)
                pe.wait_ge(wt, 1)
                for t in range(NT):
                    last = pe.transpose(DN[2 + t // 4][0:count, t % 4 * P:(t % 4 + 1) * P], WALL[:, t, :], ident[:])
                last.then_inc(turned, 1)
                pe.wait_ge(wt, 3)
                for t in range(NT):
                    last = pe.matmul(DN[t // 4][:, t % 4 * D:(t % 4 + 1) * D], WT[0:count, t * P:(t + 1) * P],
                                     B2[0:count, :], start=True, stop=True)
                last.then_inc(b2_done, 1)
                pe.wait_ge(acc0, 1)

                def body(e, par, ep):
                    down(e, par, ep)
                    up(e + 2, par, ep + 1)

                loop(pe, body)
                for e in last_two:
                    down(*e)

            @block.scalar
            def _(act):
                if normed is None:
                    act.wait_ge(r, 4)
                    act.activation(R["prob"][:], R["tmp"][:], ACT.Exp).then_inc(exp_done, 1)
                else:
                    act.wait_ge(r, 12)
                    act.activation(C["e"][:], C["neg"][:], ACT.Exp).then_inc(exp_done, 1)
                def hidden(e, par, ep):
                    for k in range(KF):
                        for half in range(2):
                            j = 2 * k + half
                            act.wait_ge(up_done, 8 * e + j + 1)
                            act.activation(H[par][:, k, half * 512:(half + 1) * 512], UP[j % 4][:], func,
                                           bias=B1[par][:, k:k + 1]).then_inc(h_done, 1)

                hidden(0, 0, 0)
                hidden(1, 1, 0)
                act.wait_ge(turned, 1)
                act.activation(WT[0:count, 512:1024], DN[3][0:count, :], ACT.Copy).then_inc(wt, 1)
                loop(act, lambda e, par, ep: hidden(e + 2, par, ep + 1))

            @block.vector
            def _(dve):
                def affine(e, par, ep):
                    dve.wait_ge(w1_in[par], PER_W * (ep + 1))
                    if not isinstance(e, int) or e >= 2:
                        dve.wait_ge(up_done, 8 * e - 7)
                    dve.tensor_scalar(XE[par][:], XT_in[:], AFF[par][:, 0:1], AFF[par][:, 1:2], ALU.mult, ALU.add)\
                       .then_inc(xe_done, 1)

                if normed is not None:
                    affine(0, 0, 0)
                    affine(1, 1, 0)
                for e in range(G):
                    dve.memset(REV[:, :, e], float(G - e))
                dve.memset(WALL[:], 1.0).then_inc(r, 1)
                steps = 1

                def then(ins):
                    nonlocal steps
                    steps += 1
                    ins.then_inc(r, 1)
                    dve.wait_ge(r, steps)

                def wide(c):
                    return c[:].unsqueeze(2).broadcast_to([P, NT, G])

                def pick(src, one, value):
                    then(dve.tensor_reduce(value[:], src[:], AX.X, ALU.max))
                    then(dve.tensor_tensor(R["eq"][:], src[:], wide(value), ALU.is_equal))
                    then(dve.tensor_tensor(R["eq"][:], R["eq"][:], REV[:], ALU.mult))
                    then(dve.tensor_reduce(C["pos"][:], R["eq"][:], AX.X, ALU.max))
                    then(dve.tensor_tensor(one[:], R["eq"][:], wide(C["pos"]), ALU.is_equal))

                dve.wait_ge(r, 1)
                dve.wait_ge(logits, 1)
                lg = DN[3][:, 0:NT * G].rearrange("p (t e) -> p t e", e=G)
                if normed is None:
                    then(dve.tensor_tensor(R["score"][:], lg, GB[:].unsqueeze(1).broadcast_to([P, NT, G]), ALU.add))
                    then(dve.tensor_reduce(C["m"][:], R["score"][:], AX.X, ALU.max))
                    then(dve.tensor_tensor(R["tmp"][:], R["score"][:], wide(C["m"]), ALU.subtract))
                    dve.wait_ge(exp_done, 1)
                    then(dve.tensor_reduce(C["den"][:], R["prob"][:], AX.X, ALU.add))
                    then(dve.reciprocal(C["rden"][:], C["den"][:]))
                    then(dve.tensor_tensor(R["score"][:], R["prob"][:], wide(C["rden"]), ALU.mult))
                    pick(R["score"], R["one1"], C["v1"])
                    then(dve.scalar_tensor_tensor(R["rest"][:], R["one1"][:], -2.0, R["score"][:], ALU.mult, ALU.add))
                    pick(R["rest"], R["one2"], C["v2"])
                    then(dve.tensor_tensor(C["sum"][:], C["v1"][:], C["v2"][:], ALU.add))
                    then(dve.tensor_scalar(C["sum"][:], C["sum"][:], 1e-9, None, ALU.add))
                    then(dve.reciprocal(C["rden"][:], C["sum"][:]))
                    then(dve.tensor_tensor(C["w1"][:], C["v1"][:], C["rden"][:], ALU.mult))
                    then(dve.tensor_tensor(C["w2"][:], C["v2"][:], C["rden"][:], ALU.mult))
                else:
                    then(dve.tensor_copy(R["score"][:], lg))
                    pick(R["score"], R["one1"], C["v1"])
                    then(dve.scalar_tensor_tensor(R["rest"][:], R["one1"][:], -3e38, R["score"][:], ALU.mult, ALU.add))
                    then(dve.tensor_reduce(C["v2"][:], R["rest"][:], AX.X, ALU.max))
                    then(dve.tensor_tensor(R["eq"][:], R["rest"][:], wide(C["v2"]), ALU.is_equal))
                    then(dve.tensor_tensor(R["eq"][:], R["eq"][:], REV[:], ALU.mult))
                    then(dve.tensor_tensor(C["neg"][:], C["v2"][:], C["v1"][:], ALU.subtract))
                    assert steps == 12
                    then(dve.tensor_reduce(C["pos"][:], R["eq"][:], AX.X, ALU.max))
                    then(dve.tensor_tensor(R["one2"][:], R["eq"][:], wide(C["pos"]), ALU.is_equal))
                    dve.wait_ge(exp_done, 1)
                    then(dve.tensor_scalar(C["den"][:], C["e"][:], 1.0, None, ALU.add))
                    then(dve.reciprocal(C["w1"][:], C["den"][:]))
                    then(dve.tensor_tensor(C["w2"][:], C["e"][:], C["w1"][:], ALU.mult))
                    then(dve.tensor_tensor(C["sum"][:], C["w1"][:], C["w2"][:], ALU.add))
                then(dve.tensor_tensor(R["one1"][:], R["one1"][:], wide(C["w1"]), ALU.mult))
                then(dve.tensor_tensor(R["one2"][:], R["one2"][:], wide(C["w2"]), ALU.mult))
                dve.tensor_tensor(WALL[:, :, 0:G], R["one1"][:], R["one2"][:], ALU.add).then_inc(wt, 1)
                dve.wait_ge(turned, 1)
                dve.tensor_copy(WT[0:count, 0:512], DN[2][0:count, :]).then_inc(wt, 1)
                dve.wait_ge(b2_done, 1)
                for g in range(2):
                    dve.tensor_copy(ACC[:, 4 * g:4 * g + 4, :],
                                    DN[g][:].rearrange("p (t d) -> p t d", d=D)).then_inc(acc_done, 1)
                dve.wait_ge(acc_done, 2)
                if normed is None:
                    dve.tensor_tensor(ACC[:], ACC[:], XH[:], ALU.add).then_inc(acc_done, 1)
                else:
                    for t in range(NT):
                        last = dve.scalar_tensor_tensor(ACC[:, t, :], XH[:, t, :], C["sum"][:, t:t + 1], ACC[:, t, :],
                                                        ALU.mult, ALU.add)
                    last.then_inc(acc_done, 1)
                dve.wait_ge(acc_done, 3)
                dve.tensor_tensor(ACC[:], ACC[:], X[:], ALU.add).then_inc(acc_done, 1)
                dve.wait_ge(acc_done, 4)
                dve.engine_nop().then_inc(acc0, 1)

                def add(e, par, ep):
                    dve.wait_ge(acc_done, 2 * e + 4)
                    dve.tensor_copy(WE[par][:], WALL[:, :, bass.ds(e, 1)].rearrange("p t e -> p (t e)"))\
                       .then_inc(x_done, 1)
                    dve.wait_ge(x_done, e + 1)
                    for g in range(2):
                        dve.wait_ge(dn_done, 2 * e + g + 1)
                        for j in range(4):
                            t = 4 * g + j
                            last = dve.scalar_tensor_tensor(ACC[:, t, :], DN[2 * par + g][:, j * D:(j + 1) * D],
                                                            WE[par][:, t:t + 1], ACC[:, t, :], ALU.mult, ALU.add)
                        last.then_inc(acc_done, 1)

                def body(e, par, ep):
                    if normed is not None:
                        affine(e + 2, par, ep + 1)
                    add(e, par, ep)

                loop(dve, body)
                for e in last_two:
                    add(*e)
                dve.wait_ge(acc_done, 2 * count + 4)
                dve.tensor_copy(X[:], ACC[:]).then_inc(x_done, 1)


def store(nc, X, out):
    with ExitStack() as ctx:
        stored = ctx.enter_context(nc.semaphore("stored"))
        with nc.Block() as block:
            @block.sync
            def _(sp):
                sp.dma_start(out.rearrange("b (t p) d -> p (b t) d", p=P), X[:]).then_inc(stored, 16)
                sp.wait_ge(stored, 16)


def build(nc, a, out, stages=None):
    with ExitStack() as held, ExitStack() as ctx:
        norms = NormSemaphores(nc, held)

        def sb(n, shape, dt=F32):
            return ctx.enter_context(nc.sbuf_tensor(n, shape, dt))

        X = sb("X", [P, NT, D])
        XT = sb("XT", [P, N])
        ident = sb("ident", [P, P])

        def norm_only(name, **kw):
            with nc.sbuf_tensor(f"{name}_XH", [P, NT, D], F32) as XH:
                layer_norm(nc, norms, name, 1e-5, X, XH, XT, ident, **kw)

        x_dram = a["x"].rearrange("b (t p) d -> p (b t) d", p=P)
        on = (lambda s: stages is None or s in stages)
        norm_only("ln0", load=[(X[:], x_dram), (ident[:], a["ident"])])
        if on("a0"):
            attention(nc, held, "a0", 16, N, X, XT, ident, [a[f"L0_attn_{n}"] for n in ("Wq", "Wk", "Wv", "Wp")],
                      a["L0_attn_bp"])
        if on("c0"):
            norm_only("ln1")
            attention(nc, held, "c0", 16, a["ctx"].shape[1], X, XT, ident,
                      [a[f"L0_xattn_{n}"] for n in ("Wq", "Wk", "Wv", "Wo")], a["L0_xattn_bo"], ctx_dram=a["ctx"])
        if on("f0"):
            with nc.sbuf_tensor("XH", [P, NT, D], F32) as XH:
                layer_norm(nc, norms, "ln2", 1e-5, X, XH, XT, ident)
                experts(nc, held, "f0", 9, 8, X, XH, XT, ident,
                        dict(gate=a["L0_ffn_gate_w"], gate_b=a["L0_ffn_gate_b"], w1=a["L0_w1"], b1=a["L0_b1"],
                             w2=a["L0_w2"], b2=a["L0_b2"]), ACT.Gelu_apprx_tanh, None)
        if on("a1"):
            norm_only("ln3")
            with nc.sbuf_tensor("VH", [P, NT, P], F32R) as VH, nc.sbuf_tensor("VL", [P, NT, P], F32R) as VL:
                scratch = {n: nc.dram_tensor(f"scratch_{n}", (16, 8, N), F32, kind="Internal").ap()
                           for n in ("qh", "ql", "kh", "kl")}
                rotary(nc, held, "rot", XT, [a[n] for n in ("L1_attn_Wq", "L1_attn_Wq_turned", "L1_attn_Wkv",
                                                      "L1_attn_Wkv_turned")],
                       [a[n] for n in ("cos", "sin", "cos_t", "sin_t")], scratch, VH, VL, float(np.float32(8 ** -0.5)))
                attention(nc, held, "a1", 16, N, X, XT, ident, [None, None, None, a["L1_attn_Wout"]], a["L1_attn_bout"],
                          packed=dict(scratch, vh=VH, vl=VL))
        if on("c1"):
            norm_only("ln4")
            attention(nc, held, "c1", 8, a["ctx"].shape[1], X, XT, ident,
                      [a[f"L1_xattn_{n}"] for n in ("Wq", "Wk", "Wv", "Wo")], a["L1_xattn_bo"], ctx_dram=a["ctx"])
        if on("f1"):
            XH = sb("XH_last", [P, NT, D])
            layer_norm(nc, norms, "ln5", 1e-5, X, XH, XT, ident)
            XH2, XT2 = sb("XH2", [P, NT, D]), sb("XT2", [P, N])
            layer_norm(nc, norms, "ln6", 1e-6, XH, XH2, XT2, ident)
            experts(nc, held, "f1", 8, 8, X, XH, XT, ident,
                    dict(gate=a["L1_ffn_Wg"], gate_b=None, w1=a["L1_w1"], b1=a["L1_b1"], w2=a["L1_w2"],
                         b2=a["L1_b2"], affine=a["L1_affine"]), ACT.Relu, XT2)
        store(nc, X, out)


def lay_out(x):
    f = np.float32
    x = {k: np.asarray(v) for k, v in x.items()}
    o = {"x": x["x"], "ctx": x["ctx_768"][0].T, "ident": np.eye(P, dtype=f)}

    def twice(w):
        return np.concatenate([w, w], axis=2)

    def split(w, h):
        return w.reshape(w.shape[0], h, -1).transpose(1, 0, 2)

    def rows_twice(w):
        out = np.zeros((w.shape[0], 2, E, w.shape[2]), f)
        out[:, :, :w.shape[1]] = w[:, None]
        return out.reshape(w.shape[0], 2 * E, w.shape[2])

    o["L0_attn_Wq"], o["L0_attn_Wk"], o["L0_attn_Wv"] = twice(x["L0_attn_Wq"]), twice(x["L0_attn_Wk"]), x["L0_attn_Wv"]
    o["L0_attn_Wp"] = rows_twice(x["L0_attn_Wp"].reshape(E, 16, D).transpose(1, 0, 2))
    for n, h in (("L0", 16), ("L1", 8)):
        for m in ("Wq", "Wk"):
            o[f"{n}_xattn_{m}"] = twice(split(x[f"{n}_xattn_{m}"], h))
        o[f"{n}_xattn_Wv"] = split(x[f"{n}_xattn_Wv"], h)
        o[f"{n}_xattn_Wo"] = rows_twice(x[f"{n}_xattn_Wo"].reshape(h, E, D))
        o[f"{n}_xattn_bo"] = x[f"{n}_xattn_bo"]
    o["L0_attn_bp"] = x["L0_attn_bp"]
    o["L0_ffn_gate_w"], o["L0_ffn_gate_b"] = x["L0_ffn_gate_w"], x["L0_ffn_gate_b"]

    def by_rows(b):
        return b.reshape(b.shape[0], -1, P).transpose(0, 2, 1)

    def by_row_tiles(w):
        return w.reshape(w.shape[0], -1, P, D).transpose(0, 2, 1, 3)

    o["L0_w1"] = np.concatenate([x["L0_ffn_ew1"], x["L0_ffn_sh_w1"][None]])
    o["L0_b1"] = by_rows(np.concatenate([x["L0_ffn_eb1"], x["L0_ffn_sh_b1"][None]]))
    o["L0_w2"] = by_row_tiles(np.concatenate([x["L0_ffn_ew2"], x["L0_ffn_sh_w2"][None]]))
    o["L0_b2"] = np.concatenate([x["L0_ffn_eb2"], x["L0_ffn_sh_b2"][None]])
    perm = np.arange(P).reshape(16, 2, 4)[:, ::-1].reshape(P)
    for n in ("Wq", "Wkv"):
        o[f"L1_attn_{n}"], o[f"L1_attn_{n}_turned"] = x[f"L1_attn_{n}"], x[f"L1_attn_{n}"][:, perm]
    o["L1_attn_Wout"] = rows_twice(x["L1_attn_Wout"].reshape(16, 8, D))
    o["L1_attn_bout"] = x["L1_attn_bout"]
    freq = f(1.0) / f(10000.0) ** (np.arange(0, 8, 2, dtype=f) / f(8))
    angle = np.outer(np.arange(N, dtype=f), freq).astype(f)
    cos = np.tile(np.cos(angle), (1, 2 * 16)).astype(f)
    sin = np.tile(np.concatenate([-np.sin(angle), np.sin(angle)], axis=1), (1, 16)).astype(f)
    o["cos_t"], o["sin_t"], o["cos"], o["sin"] = cos, sin, cos.T, sin.T
    o["L1_ffn_Wg"] = x["L1_ffn_Wg"]
    o["L1_w1"], o["L1_b1"] = x["L1_ffn_W1"], by_rows(x["L1_ffn_b1"])
    o["L1_w2"], o["L1_b2"] = by_row_tiles(x["L1_ffn_W2"]), x["L1_ffn_b2"]
    o["L1_affine"] = np.stack([x["L1_ffn_gamma"], x["L1_ffn_beta"]], axis=2)
    return {k: np.ascontiguousarray(v) for k, v in o.items()}


def kernel(**inputs):
    import concourse.bacc as bacc
    from concourse.bass_utils import run_bass_kernel_spmd

    arrays = lay_out(inputs)
    nc = bacc.Bacc("TRN2", target_bir_lowering=False, num_devices=1, dynamic_dma_scratch_size=1024)
    aps = {n: nc.dram_tensor(f"in_{n}", v.shape, mybir.dt.from_np(v.dtype), kind="ExternalInput").ap()
           for n, v in arrays.items()}
    out = nc.dram_tensor("out", (1, N, D), F32, kind="ExternalOutput").ap()
    build(nc, aps, out)
    r = run_bass_kernel_spmd(nc, [{f"in_{n}": v for n, v in arrays.items()}], core_ids=[0])
    return r.results[0]["out"]
```
